# Optimizing a Trainium2 kernel written in Bass

```python
import numpy as np
import jax
import jax.numpy as jnp

def _softmax(x, axis=-1):
    return jax.nn.softmax(x, axis=axis)

def _gelu(x):
    return jax.nn.gelu(x, approximate=True)

def _silu(x):
    return jax.nn.silu(x)

def _sigmoid(x):
    return jax.nn.sigmoid(x)

def _layernorm(x, axis=-1, eps=1e-05):
    m = jnp.mean(x, axis=axis, keepdims=True)
    v = jnp.var(x, axis=axis, keepdims=True)
    return (x - m) / jnp.sqrt(v + eps)

def _scatter_add(tgt, idx, src, axis=0):
    return tgt.at[idx].add(src)

def _segment_sum(src, seg, n):
    return jax.ops.segment_sum(src, seg, n)
kernel_name = 'mk_adj_preln_d4_adj_r2_355938'

def setup_inputs(seed: int=0):
    np.random.seed(seed)
    _w = jnp.asarray

    def _rec_inputs():
        import jax
        import jax.numpy as jnp
        _gk = jax.random.key(seed)
        x = 7.22e-05 + 1 * jax.random.normal(jax.random.fold_in(_gk, 1), (32, 256, 256), jnp.float32)
        _a = jax.random.bernoulli(jax.random.fold_in(_gk, 2), 0.0625, (32, 256, 256))
        _a = jnp.logical_or(_a, jnp.swapaxes(_a, -1, -2))
        _a = jnp.logical_or(_a, jnp.eye(256, dtype=bool))
        _af = _a.astype(jnp.float32)
        adj = _af
        return (x, adj)
    x, adj = _rec_inputs()

    def _L0_gnn_setup():
        import jax, jax.numpy as jnp
        import numpy as np
        IN_DIM = 256
        ATT_DIM = 64
        B, N = (4, 2048)
        key = jax.random.key(seed)
        k1, k2, k3, k4 = jax.random.split(key, 4)
        x = jax.random.normal(k1, (B, N, IN_DIM), dtype=jnp.float32)
        adj_matrix = (jax.random.uniform(k2, (B, N, N)) < 0.05).astype(jnp.float32)
        W_qk = jax.random.normal(k3, (2 * ATT_DIM, IN_DIM), dtype=jnp.float32) / np.sqrt(IN_DIM)
        W_v = jax.random.normal(k4, (IN_DIM, IN_DIM), dtype=jnp.float32) / np.sqrt(IN_DIM)
        return {'x': x, 'adj_matrix': adj_matrix, 'W_qk': W_qk, 'W_v': W_v}
    _L0_gnn_all = _L0_gnn_setup()
    _L0_gnn_in = {k: v for k, v in _L0_gnn_all.items() if k in ('W_qk', 'W_v')}
    del _L0_gnn_all

    def _L1_gnn_setup():
        import jax, jax.numpy as jnp
        import numpy as np
        EMBED_DIM = 256
        NUM_HEADS = 8
        HEAD_DIM = EMBED_DIM // NUM_HEADS
        SCALE = HEAD_DIM ** (-0.5)
        B, S = (16, 512)
        key = jax.random.key(seed)
        ks = jax.random.split(key, 12)
        init = lambda k, shape: jax.random.normal(k, shape, dtype=jnp.float32) * EMBED_DIM ** (-0.5)
        return {'x': jax.random.normal(ks[0], (B, S, EMBED_DIM), dtype=jnp.float32), 'adj_matrix': jax.random.uniform(ks[1], (B, S, S), dtype=jnp.float32), 'bond_matrix': jax.random.uniform(ks[2], (B, S, S), dtype=jnp.float32), 'Wq': init(ks[3], (EMBED_DIM, EMBED_DIM)), 'bq': jnp.zeros((EMBED_DIM,), jnp.float32), 'Wk': init(ks[4], (EMBED_DIM, EMBED_DIM)), 'bk': jnp.zeros((EMBED_DIM,), jnp.float32), 'Wv': init(ks[5], (EMBED_DIM, EMBED_DIM)), 'bv': jnp.zeros((EMBED_DIM,), jnp.float32), 'Wo': init(ks[6], (EMBED_DIM, EMBED_DIM)), 'bo': jnp.zeros((EMBED_DIM,), jnp.float32), 'seq_len': S}
    _L1_gnn_all = _L1_gnn_setup()
    _L1_gnn_in = {k: v for k, v in _L1_gnn_all.items() if k in ('Wq', 'bq', 'Wk', 'bk', 'Wv', 'bv', 'Wo', 'bo')}
    del _L1_gnn_all

    def _L2_gnn_setup():
        import jax, jax.numpy as jnp
        import numpy as np
        B, N, C_IN, C_OUT = (8, 2048, 256, 256)
        key = jax.random.key(seed)
        k1, k2, k3, k4 = jax.random.split(key, 4)
        node_features = jax.random.normal(k1, (B, N, C_IN), dtype=jnp.float32)
        adj_matrix = jax.random.uniform(k2, (B, N, N), dtype=jnp.float32)
        W = jax.random.normal(k3, (C_IN, C_OUT), dtype=jnp.float32) / np.sqrt(C_IN)
        b = jax.random.normal(k4, (C_OUT,), dtype=jnp.float32) * 0.01
        return {'node_features': node_features, 'adj_matrix': adj_matrix, 'W': W, 'b': b}
    _L2_gnn_all = _L2_gnn_setup()
    _L2_gnn_in = {k: v for k, v in _L2_gnn_all.items() if k in ('W', 'b')}
    del _L2_gnn_all

    def _L3_gnn_setup():
        import jax, jax.numpy as jnp
        import numpy as np
        B, N, DIN, DOUT, K = (4, 1024, 256, 256, 3)
        key = jax.random.key(seed)
        ks = jax.random.split(key, 8)
        X = jax.random.normal(ks[0], (B, N, DIN), dtype=jnp.float32)
        A = jax.random.uniform(ks[1], (B, N, N), dtype=jnp.float32)
        Wv = jax.random.normal(ks[2], (DIN, DOUT), dtype=jnp.float32) * 0.02
        bv = jax.random.normal(ks[3], (DOUT,), dtype=jnp.float32) * 0.02
        aw = jax.random.normal(ks[4], (2 * DOUT, 1), dtype=jnp.float32) * 0.05
        ab = jax.random.normal(ks[5], (1,), dtype=jnp.float32) * 0.05
        Wk = jax.random.normal(ks[6], (K, DIN, DOUT), dtype=jnp.float32) * 0.02
        bk = jax.random.normal(ks[7], (K, DOUT), dtype=jnp.float32) * 0.02
        return {'X': X, 'A': A, 'Wv': Wv, 'bv': bv, 'aw': aw, 'ab': ab, 'Wk': Wk, 'bk': bk}
    _L3_gnn_all = _L3_gnn_setup()
    _L3_gnn_in = {k: v for k, v in _L3_gnn_all.items() if k in ('Wv', 'bv', 'aw', 'ab', 'Wk', 'bk')}
    del _L3_gnn_all
    return {'x': x, 'adj': adj, 'L0_gnn_W_qk': _L0_gnn_in['W_qk'], 'L0_gnn_W_v': _L0_gnn_in['W_v'], 'L1_gnn_Wq': _L1_gnn_in['Wq'], 'L1_gnn_bq': _L1_gnn_in['bq'], 'L1_gnn_Wk': _L1_gnn_in['Wk'], 'L1_gnn_bk': _L1_gnn_in['bk'], 'L1_gnn_Wv': _L1_gnn_in['Wv'], 'L1_gnn_bv': _L1_gnn_in['bv'], 'L1_gnn_Wo': _L1_gnn_in['Wo'], 'L1_gnn_bo': _L1_gnn_in['bo'], 'L2_gnn_W': _L2_gnn_in['W'], 'L2_gnn_b': _L2_gnn_in['b'], 'L3_gnn_Wv': _L3_gnn_in['Wv'], 'L3_gnn_bv': _L3_gnn_in['bv'], 'L3_gnn_aw': _L3_gnn_in['aw'], 'L3_gnn_ab': _L3_gnn_in['ab'], 'L3_gnn_Wk': _L3_gnn_in['Wk'], 'L3_gnn_bk': _L3_gnn_in['bk']}

def reference(x, adj, L0_gnn_W_qk, L0_gnn_W_v, L1_gnn_Wq, L1_gnn_bq, L1_gnn_Wk, L1_gnn_bk, L1_gnn_Wv, L1_gnn_bv, L1_gnn_Wo, L1_gnn_bo, L2_gnn_W, L2_gnn_b, L3_gnn_Wv, L3_gnn_bv, L3_gnn_aw, L3_gnn_ab, L3_gnn_Wk, L3_gnn_bk):
    import jax
    import jax.numpy as jnp

    def _L0_gnn_ref(x, adj_matrix, W_qk, W_v):
        import jax, jax.numpy as jnp
        import numpy as np
        IN_DIM = 256
        ATT_DIM = 64
        B, N = (4, 2048)
        qk = jnp.einsum('bnd,ed->bne', x, W_qk)
        q, k = jnp.split(qk, 2, axis=-1)
        v = jnp.einsum('bnd,ed->bne', x, W_v)
        inv_scale = 1.0 / ATT_DIM ** 0.5
        scores = jnp.einsum('bnd,bmd->bnm', q, k) * inv_scale
        w = jnp.sum(scores * adj_matrix, axis=-1, keepdims=True)
        w = jax.nn.softmax(w, axis=1)
        return w * v

    def _L1_gnn_ref(x, adj_matrix, bond_matrix, Wq, bq, Wk, bk, Wv, bv, Wo, bo, seq_len):
        import jax, jax.numpy as jnp
        import numpy as np
        EMBED_DIM = 256
        NUM_HEADS = 8
        HEAD_DIM = EMBED_DIM // NUM_HEADS
        SCALE = HEAD_DIM ** (-0.5)
        B, S = (16, 512)
        b = x.shape[0]

        def proj(W, bias):
            y = jnp.einsum('bse,fe->bsf', x, W) + bias
            return y.reshape(b, seq_len, NUM_HEADS, HEAD_DIM).transpose(0, 2, 1, 3)
        q, k, v = (proj(Wq, bq), proj(Wk, bk), proj(Wv, bv))
        scores = jnp.einsum('bhqd,bhkd->bhqk', q, k) * SCALE
        mask = (adj_matrix + bond_matrix)[:, None, :, :]
        scores = scores * mask
        attn = jax.nn.softmax(scores, axis=-1)
        ctx = jnp.einsum('bhqk,bhkd->bhqd', attn, v)
        ctx = ctx.transpose(0, 2, 1, 3).reshape(b, seq_len, EMBED_DIM)
        return jnp.einsum('bse,fe->bsf', ctx, Wo) + bo

    def _L2_gnn_ref(node_features, adj_matrix, W, b):
        import jax, jax.numpy as jnp
        import numpy as np
        B, N, C_IN, C_OUT = (8, 2048, 256, 256)
        num_neighbours = adj_matrix.sum(axis=-1, keepdims=True)
        h = jnp.einsum('bni,io->bno', node_features, W) + b
        h = jnp.einsum('bnm,bmo->bno', adj_matrix, h)
        return h / num_neighbours

    def _L3_gnn_ref(X, A, Wv, bv, aw, ab, Wk, bk):
        import jax, jax.numpy as jnp
        import numpy as np
        B, N, DIN, DOUT, K = (4, 1024, 256, 256, 3)
        d = Wv.shape[1]
        Xw = X @ Wv + bv
        sj = Xw @ aw[:d, 0]
        si = Xw @ aw[d:, 0]
        e = jax.nn.leaky_relu(sj[:, None, :] + si[:, :, None] + ab[0], negative_slope=0.2)
        alpha_matrix = A * jnp.exp(e)
        transition = alpha_matrix / (jnp.sum(alpha_matrix, axis=-1, keepdims=True) + 1e-12)
        H = jnp.zeros(X.shape[:-1] + (d,), dtype=X.dtype)
        Xk = X
        for k in range(Wk.shape[0]):
            H = H + Xk @ Wk[k] + bk[k]
            Xk = jnp.einsum('bij,bjd->bid', transition, Xk)
        return jax.nn.relu(H)
    h = jnp.maximum(_layernorm(x, axis=-1), 0.0)
    x = x + _L0_gnn_ref(h, adj, L0_gnn_W_qk, L0_gnn_W_v)
    h = jnp.maximum(_layernorm(x, axis=-1), 0.0)
    x = x + _L1_gnn_ref(h, adj, adj, L1_gnn_Wq, L1_gnn_bq, L1_gnn_Wk, L1_gnn_bk, L1_gnn_Wv, L1_gnn_bv, L1_gnn_Wo, L1_gnn_bo, 256)
    h = jnp.maximum(_layernorm(x, axis=-1), 0.0)
    x = x + _L2_gnn_ref(h, adj, L2_gnn_W, L2_gnn_b)
    h = jnp.maximum(_layernorm(x, axis=-1), 0.0)
    x = x + _L3_gnn_ref(h, adj, L3_gnn_Wv, L3_gnn_bv, L3_gnn_aw, L3_gnn_ab, L3_gnn_Wk, L3_gnn_bk)
    return x

_drawn_inputs = setup_inputs


def setup_inputs(seed=0):
    import zlib

    import numpy as np

    out = dict(_drawn_inputs(seed))
    spreads = {'L1_gnn_bq': (0.0, 0.8),
     'L1_gnn_bk': (0.0, 0.8),
     'L1_gnn_bv': (0.0, 0.1),
     'L1_gnn_bo': (0.0, 0.1)}
    factors = {'L1_gnn_Wk': 2.828,
     'L2_gnn_b': 7.188,
     'L3_gnn_Wv': 8.0,
     'L3_gnn_bv': 64.0,
     'L3_gnn_aw': 8.0,
     'L3_gnn_bk': 3.081}
    for name, (base, spread) in spreads.items():
        noise = np.random.default_rng([zlib.crc32(name.encode()), seed]).standard_normal(out[name].shape)
        drawn = base * np.exp(spread * noise) if base else spread * noise
        out[name] = jnp.asarray(drawn.astype(out[name].dtype))
    for name, factor in factors.items():
        out[name] = (out[name] * factor).astype(out[name].dtype)
    return out
```

```python
from contextlib import ExitStack

import concourse.bass as bass
from concourse import mybir

F32 = mybir.dt.float32
F32R = mybir.dt.float32r
ALU = mybir.AluOpType
ACT = mybir.ActivationFunctionType
AX_X = mybir.AxisListType.X

P = 128
BODY = 4
SLOTS = 14
DEPTH = 4
LEAST = -3.0e38

LOAD = 0
NORM0, XT0, ADJ_T, QK0, EDGE_SUM, W_ALL, W_PROB, V0 = 3, 5, 6, 7, 8, 9, 10, 11
XT1, Q1, K1, V1 = 14, 15, 16, 17
HEAD, TURN, CONTEXT = 27, 29, 30
C_COLS, X2 = 39, 40
XT2, H2, NEAR = 43, 44, 45
XT3, EDGE, ALPHA, XW2, XW1, HOP1, XW0, HOP2 = 48, 49, 50, 51, 52, 53, 54, 55


class Graph:

    def __init__(self, i, c):
        self.i, self.c = i, c
        self.two, self.four = c % 2, c % 4
        self.first = isinstance(i, int) and c == 0

    def number(self):
        return BODY * self.i + self.c

    def count(self, each=1, events=1):
        return BODY * each * self.i + (each * self.c + events)

    def round(self, ring, each):
        return each * (BODY // ring) * self.i + each * (self.c // ring + 1)

    def before(self, n=1):
        return Graph(self.i, self.c - n)


def graph_layers_kernel(nc, x, adj, w_qk0, w_v0, w_q1, b_q1, w_k1, b_k1, w_v1, b_v1, w_o1, b_o1,
                        w2, b2, w_v3, b_v3, a_w3, a_b3, w_k3, b_k3, out):
    G, N, D = x.shape
    NT, KT = N // P, D // P
    Q0 = w_qk0.shape[1] // 2
    H = 8
    HD = D // H
    HE = HD + 1
    HG = P // HD
    HOPS = w_k3.shape[0]
    SCALE0 = float(Q0) ** -0.5
    SCALE1 = 2.0 * float(HD) ** -0.5
    ALL = G + DEPTH - 1
    AHEAD, BEHIND = DEPTH, DEPTH - 1
    ROUNDS = (ALL - AHEAD - BEHIND) // BODY
    assert (ALL - AHEAD - BEHIND) % BODY == 0 and NT == 2 and KT == 2

    with ExitStack() as ctx:
        def sb(name, shape, dt=F32):
            return ctx.enter_context(nc.sbuf_tensor(name, shape, dt))

        def bank(name):
            return ctx.enter_context(nc.psum_tensor(name, [P, 512], F32))

        def sem(name):
            return ctx.enter_context(nc.semaphore(name))

        x0 = sb("x0", [P, 2, NT, D])
        adj_n = sb("adj_n", [P, 4, NT, N])
        adj_t = sb("adj_t", [P, 4, NT, N])
        x1_bias = sb("x1_bias", [P, 4, NT, D])
        near_inv = sb("near_inv", [P, 4, NT])
        q_stack = sb("q_stack", [P, 2, H, N], F32R)
        k_stack = sb("k_stack", [P, 2, H, N], F32R)
        v_heads = sb("v_heads", [P, 2, NT, H, HE])
        x_out = sb("x_out", [P, NT, D])

        x1 = sb("x1", [P, NT, D])
        qk0 = sb("qk0", [P, NT, 2 * Q0 + 1])
        qak = sb("qak", [P, NT, Q0])
        w_col = sb("w_col", [P, NT])
        w_neg = sb("w_neg", [P, 2])
        w_exp = sb("w_exp", [P, N])
        w_sum = sb("w_sum", [P, 2])
        w_e = sb("w_e", [P, NT])
        w_prob = sb("w_prob", [P, NT])
        q_hl = sb("q_hl", [P, 2, KT, N], F32R)
        k_hl = sb("k_hl", [P, 2, KT, N], F32R)

        heads = sb("heads", [P, 9, NT * N])
        masked, centred, probs = heads[:, 0:3, :], heads[:, 3:6, :], heads[:, 6:9, :]
        s_top = sb("s_top", [P, 3, NT])
        c_inv = sb("c_inv", [P, NT, H])
        c_rows = sb("c_rows", [P, NT, H, HD])
        c_cols = sb("c_cols", [P, KT, N])
        x2 = sb("x2", [P, NT, D])
        x2_bias = sb("x2_bias", [P, NT, D])

        h2 = sb("h2", [P, NT, D])
        x3 = sb("x3", [P, NT, D])
        e_bias = sb("e_bias", [P, NT, 2])
        edges = sb("edges", [P, 4, NT, N])
        e_pos, e_leak, e_max, alpha = (edges[:, n] for n in range(4))
        a_inv = sb("a_inv", [P, 2, NT])
        xw2 = sb("xw2", [P, NT, D])
        xw1 = sb("xw1", [P, NT, D])
        xw0 = sb("xw0", [P, NT, D])
        xw0_bias = sb("xw0_bias", [P, NT, D])
        y1 = sb("y1", [P, NT, D])
        hid = sb("hid", [P, NT, D])

        x_norm = [sb(f"x_norm{n}", [P, NT, D]) for n in range(2)]
        xt_hl = [sb(f"xt_hl{n}", [P, 2, KT, N], F32R) for n in range(2)]
        stats = [sb(f"stats{n}", [P, NT, 6]) for n in range(4)]
        moments = [sb(f"moments{n}", [P, NT, 2]) for n in range(4)]
        spread = [sb(f"spread{n}", [P, 3, NT]) for n in range(4)]

        wide = {"qk0": 2 * Q0, "v0": D, "q1": D, "k1": D, "v1": D, "n2": D, "h0": D, "h1": D, "h2": D}
        w_hl = {k: sb("w_" + k, [P, 2, KT, n], F32R) for k, n in wide.items()}
        w_src = {"qk0": w_qk0, "v0": w_v0, "q1": w_q1, "k1": w_k1, "v1": w_v1, "n2": w2,
                 "h0": w_k3[0], "h1": w_k3[1], "h2": w_k3[2]}
        wo_sb = sb("wo_sb", [P, KT, D])
        si_hl = sb("si_hl", [P, 2, KT, P], F32R)
        sj_hl = sb("sj_hl", [P, 2, KT, 2], F32R)
        bo_row = sb("bo_row", [P, D])
        bv_row = sb("bv_row", [P, D])
        b2_row = sb("b2_row", [P, D])
        bk_row = sb("bk_row", [P, D])
        bqk_col = sb("bqk_col", [P, 2, KT])
        e_const = sb("e_const", [P, NT, 2])
        a_part = sb("a_part", [P, 8])
        ident = sb("ident", [P, P])
        ones = sb("ones", [P, P])
        half = sb("half", [P, NT])

        bank_s = [bank("bank_s0"), bank("bank_s1")]
        bank_t = [bank("bank_t0"), bank("bank_t1")]
        bank_c = bank("bank_c")
        bank_a = bank("bank_a")
        bank_b = bank("bank_b")
        bank_g = bank("bank_g")
        ctx_ps = bank_c[:, 0:NT * HG * HE].rearrange("p (t h e) -> p t h e", t=NT, h=HG)

        def tiles(b):
            return b[:, :].rearrange("p (t n) -> p t n", t=2)

        s_weights = sem("s_weights")
        s_rows = sem("s_rows")
        s_made = sem("s_made")
        s_ident = sem("s_ident")
        s_setup = sem("s_setup")
        s_carry = sem("s_carry")
        s_x = [sem(f"s_x_in{n}") for n in range(2)]
        s_adj = [sem(f"s_adj_in{n}") for n in range(4)]
        s_stats = [sem(f"s_stats{n}") for n in range(4)]
        s_moments = [sem(f"s_moments{n}") for n in range(4)]
        s_spread = [sem(f"s_spread{n}") for n in range(4)]
        s_norm = [sem(f"s_norm{n}") for n in range(4)]
        s_xt_ps = [sem(f"s_xt_ps{n}") for n in range(4)]
        s_xt_hi = [sem(f"s_xt_hi{n}") for n in range(4)]
        s_xt = [sem(f"s_xt{n}") for n in range(4)]
        s_adj_ps, s_adj_t = sem("s_adj_ps"), sem("s_adj_t")
        s_qk0_ps, s_qk0 = sem("s_qk0_ps"), sem("s_qk0")
        s_ak_ps, s_w_col = sem("s_ak_ps"), sem("s_w_col")
        s_w_max = sem("s_w_max")
        s_w_ps, s_w_neg, s_w_exp, s_w_inv, s_w_prob = (
            sem("s_w_ps"), sem("s_w_neg"), sem("s_w_exp"), sem("s_w_inv"), sem("s_w_prob"))
        s_v0_ps, s_x1, s_x1_bias = sem("s_v0_ps"), sem("s_x1"), sem("s_x1_bias")
        s_q1_ps, s_q1_hi, s_q1 = sem("s_q1_ps"), sem("s_q1_hi"), sem("s_q1")
        s_k1_ps, s_k1_hi, s_k1 = sem("s_k1_ps"), sem("s_k1_hi"), sem("s_k1")
        s_v1_ps, s_v1 = sem("s_v1_ps"), sem("s_v1")
        s_stack = sem("s_stack")
        s_scores, s_masked, s_centred, s_scores_t, s_probs, s_context = (
            sem("s_scores"), sem("s_masked"), sem("s_centred"), sem("s_scores_t"), sem("s_probs"),
            sem("s_context"))
        s_c_inv, s_c_rows, s_cols_ps, s_c_cols, s_x2_ps, s_x2, s_x2_bias = (
            sem("s_c_inv"), sem("s_c_rows"), sem("s_cols_ps"), sem("s_c_cols"), sem("s_x2_ps"),
            sem("s_x2"), sem("s_x2_bias"))
        s_h2_ps, s_h2, s_ah_ps, s_x3 = sem("s_h2_ps"), sem("s_h2"), sem("s_ah_ps"), sem("s_x3")
        s_e_ps, s_e_bias, s_e, s_e_max, s_alpha = (
            sem("s_e_ps"), sem("s_e_bias"), sem("s_e"), sem("s_e_max"), sem("s_alpha"))
        s_a_ps, s_a_sum, s_a_inv = sem("s_a_ps"), sem("s_a_sum"), sem("s_a_inv")
        s_xw2_ps, s_xw2, s_xw1_ps, s_xw1, s_xw0_ps, s_xw0, s_xw0_bias = (
            sem("s_xw2_ps"), sem("s_xw2"), sem("s_xw1_ps"), sem("s_xw1"), sem("s_xw0_ps"),
            sem("s_xw0"), sem("s_xw0_bias"))
        s_y2_ps, s_y1, s_hop_ps, s_hid, s_out = (
            sem("s_y2_ps"), sem("s_y1"), sem("s_hop_ps"), sem("s_hid"), sem("s_out"))
        s_stored = sem("s_stored")

        block = ctx.enter_context(nc.Block())

        def due(i, t, s):
            inside = not isinstance(i, int)
            return [(n * SLOTS + s, Graph(i, t - n)) for n in range(DEPTH) if inside or 0 <= t - n < G]

        def settled(eng):
            eng.sem_inc(s_carry, 1)

        def flat(ap):
            return ap.rearrange("p t n -> p (t n)")

        qk0_ps = bank_a[:, 0:NT * 2 * Q0].rearrange("p (t n) -> p t n", t=NT)
        ak_ps = bank_a[:, 0:NT * (Q0 + 1)].rearrange("p (t n) -> p t n", t=NT)
        hid_rows = [flat(hid[:, :, :])[:, 0:D], flat(hid[:, :, :])[:, D:2 * D], flat(y1[:, :, :])[:, 0:D]]
        STACK = 2 * HG * HG * 16

        @block.sync
        def _(sp):
            for name, src in w_src.items():
                n = list(wide).index(name)
                dst = heads[:, n, 0:KT * wide[name]].rearrange("p (k n) -> p k n", k=KT)
                sp.dma_start(dst, src.rearrange("(k p) n -> p k n", p=P)).then_inc(s_weights, 16)
            sp.dma_start(wo_sb[:, :, :], w_o1.rearrange("(k p) n -> p k n", p=P)).then_inc(s_weights, 16)
            sp.dma_start(e_pos, w_v3.rearrange("(k p) n -> p k n", p=P)).then_inc(s_rows, 16)
            sp.dma_start(e_leak, a_w3.rearrange("(o t n) u -> o t (n u)", o=1, t=2).broadcast_to([P, 2, D])).then_inc(s_rows, 16)
            sp.dma_start(e_max[:, 0], b_v3.rearrange("(o n) -> o n", o=1).broadcast_to([P, D])).then_inc(s_rows, 16)
            sp.dma_start(a_part[:, 7:8], a_b3.rearrange("(o n) -> o n", o=1).broadcast_to([P, 1])).then_inc(s_rows, 16)
            for row, src in ((bo_row, b_o1), (bv_row, b_v1), (b2_row, b2)):
                sp.dma_start(row[:, :], src.rearrange("(o n) -> o n", o=1).broadcast_to([P, D])).then_inc(s_rows, 16)
            for n in range(HOPS):
                sp.dma_start(hid_rows[n], b_k3[n:n + 1, :].broadcast_to([P, D])).then_inc(s_rows, 16)
            for n, src in enumerate((b_q1, b_k1)):
                sp.dma_start(bqk_col[:, n, :], src.rearrange("(k p) -> p k", p=P),
                             allow_slow_non_contiguous=True).then_inc(s_rows, 16)

            def load(g):
                if g.c >= 2:
                    sp.wait_ge(s_x1, g.before(2).count())
                    settled(sp)
                at = bass.ds(g.number(), 1)
                sp.dma_start(x0[:, g.two, :, :], x[at].rearrange("a (t p) d -> p (a t) d", p=P))\
                    .then_inc(s_x[g.two], 16)
                sp.dma_start(adj_n[:, g.four, :, :], adj[at].rearrange("a (t p) d -> p (a t) d", p=P))\
                    .then_inc(s_adj[g.four], 16)

            def stack(g, src, dst, order):
                for j in range(HG):
                    for c in range(HG):
                        sp.dma_start(
                            dst[c * HD:(c + 1) * HD, g.two, j::HG, :].bitcast(F32),
                            src[j * HD:(j + 1) * HD, order[c], :, :].bitcast(F32)).then_inc(s_stack, 16)

            def store(g):
                sp.wait_ge(s_out, g.count())
                settled(sp)
                at = bass.ds(g.number(), 1)
                sp.dma_start(out[at].rearrange("a (t p) d -> p (a t) d", p=P), x_out[:, :, :]).then_inc(s_stored, 16)

            def iteration(i, t):
                for s in range(SLOTS):
                    for slot, g in due(i, t, s):
                        if slot == LOAD:
                            load(g)
                        if slot == Q1:
                            sp.wait_ge(s_q1, g.count())
                            settled(sp)
                            stack(g, q_hl, q_stack, [0, 1, 0, 1])
                        if slot == K1:
                            sp.wait_ge(s_k1, g.count())
                            settled(sp)
                            stack(g, k_hl, k_stack, [0, 0, 1, 1])
                        if slot == HOP2:
                            store(g)

            for t in range(AHEAD):
                iteration(0, t)
            with sp.Fori(0, ROUNDS) as i:
                for u in range(BODY):
                    iteration(i, AHEAD + u)
            for t in range(ALL - BEHIND, ALL):
                iteration(0, t)
            sp.wait_ge(s_stored, 16 * G)

        @block.gpsimd
        def _(pool):
            nc.gpsimd.memset(ident[:, :], 0.0).then_inc(s_ident, 1)
            nc.gpsimd.memset(half[:, :], -0.5)
            pool.wait_ge(s_ident, 1)
            nc.gpsimd.affine_select(out=ident[:, :], in_=ident[:, :], compare_op=ALU.not_equal, fill=1.0,
                                    base=0, pattern=[[-1, P]], channel_multiplier=1).then_inc(s_ident, 1)
            pool.wait_ge(s_setup, 1)

            def normalise(n, g, src):
                by, mv, dst = spread[n], moments[n], x_norm[n // 2]
                nc.gpsimd.tensor_scalar(by[:, 0, :], mv[:, :, 1], 1e-5, 1.0, ALU.add, ALU.mult).then_inc(s_spread[n], 1)
                nc.gpsimd.tensor_scalar(by[:, 1, :], mv[:, :, 0], -1.0, 0.0, ALU.mult, ALU.add).then_inc(s_spread[n], 1)
                pool.wait_ge(s_spread[n], g.count(3, 2))
                nc.gpsimd.tensor_tensor(by[:, 2, :], by[:, 0, :], half[:, :], ALU.pow).then_inc(s_spread[n], 1)
                pool.wait_ge(s_spread[n], g.count(3, 3))
                settled(pool)
                for r in range(NT):
                    last = nc.gpsimd.tensor_scalar(dst[:, r, :], src[:, r, :], by[:, 1, r:r + 1], by[:, 2, r:r + 1],
                                                   ALU.add, ALU.mult)
                last.then_inc(s_norm[n], 1)

            def add_row(dst, src, row, done):
                for r in range(NT):
                    last = nc.gpsimd.tensor_tensor(dst[:, r, :], src[:, r, :], row[:, :], ALU.add)
                last.then_inc(done, 1)

            def centre(g, h):
                pool.wait_ge(s_masked, g.count(H, h + 1))
                settled(pool)
                for r in range(NT):
                    at = slice(r * N, (r + 1) * N)
                    last = nc.gpsimd.tensor_scalar(centred[:, h % 3, at], masked[:, h % 3, at], -1.0,
                                                   s_top[:, h % 3, r:r + 1], ALU.mult, ALU.add)
                last.then_inc(s_centred, 1)

            def iteration(i, t):
                for s in range(SLOTS):
                    for slot, g in due(i, t, s):
                        if 0 <= slot - HEAD < H:
                            centre(g, slot - HEAD)
                    for slot, g in due(i, t, s):
                        if slot == NORM0:
                            pool.wait_ge(s_moments[0], g.count())
                            settled(pool)
                            normalise(0, g, x0[:, g.two])
                        if slot == V0:
                            pool.wait_ge(s_moments[1], g.count())
                            settled(pool)
                            normalise(1, g, x1)
                            add_row(x1_bias[:, g.four], x1, bo_row, s_x1_bias)
                        if slot == X2:
                            pool.wait_ge(s_moments[2], g.count())
                            settled(pool)
                            normalise(2, g, x2)
                            add_row(x2_bias, x2, b2_row, s_x2_bias)
                        if slot == NEAR:
                            pool.wait_ge(s_moments[3], g.count())
                            settled(pool)
                            normalise(3, g, x3)
                        if slot == ALPHA:
                            pool.wait_ge(s_e_max, g.count())
                            nc.gpsimd.tensor_tensor(alpha, e_max, adj_t[:, g.four], ALU.mult).then_inc(s_alpha, 1)
                        if slot == XW0:
                            pool.wait_ge(s_xw0, g.count())
                            add_row(xw0_bias, xw0, bk_row, s_xw0_bias)

            for t in range(AHEAD):
                iteration(0, t)
            with pool.Fori(0, ROUNDS) as i:
                for u in range(BODY):
                    iteration(i, AHEAD + u)
            for t in range(ALL - BEHIND, ALL):
                iteration(0, t)

        @block.scalar
        def _(act):
            act.wait_ge(s_setup, 1)

            def relu_hi(n, src):
                nc.scalar.activation(flat(xt_hl[n // 2][:, 0]), src[:, :], ACT.Relu).then_inc(s_xt_hi[n], 1)

            def bias_hi(dst, col, done):
                for k in range(KT):
                    last = nc.scalar.activation(dst[:, 0, k, :], tiles(bank_a)[:, k], ACT.Identity,
                                                bias=bqk_col[:, col, k:k + 1])
                last.then_inc(done, 1)

            def iteration(i, t):
                for s in range(SLOTS):
                    for slot, g in due(i, t, s):
                        if slot == XT0:
                            act.wait_ge(s_xt_ps[0], g.count())
                            relu_hi(0, bank_a)
                        if slot == ADJ_T:
                            act.wait_ge(s_adj_ps, g.count())
                            nc.scalar.activation(adj_t[:, g.four], tiles(bank_a), ACT.Copy).then_inc(s_adj_t, 1)
                        if slot == W_PROB:
                            act.wait_ge(s_w_neg, g.count())
                            nc.scalar.activation(w_exp[:, :], bank_a[:, 0:N], ACT.Exp, bias=w_neg[:, 1:2], scale=SCALE0,
                                                 accum_out=w_sum[:, 0:1])
                            nc.scalar.activation(w_e[:, :], w_col[:, :], ACT.Exp, bias=w_neg[:, 1:2], scale=SCALE0)\
                                .then_inc(s_w_exp, 1)
                        if slot == XT1:
                            act.wait_ge(s_xt_ps[1], g.count())
                            relu_hi(1, bank_a)
                        if slot == Q1:
                            act.wait_ge(s_q1_ps, g.count())
                            if not g.first:
                                act.wait_ge(s_stack, g.before().count(STACK, STACK))
                            bias_hi(q_hl, 0, s_q1_hi)
                        if slot == K1:
                            act.wait_ge(s_k1_ps, g.count())
                            bias_hi(k_hl, 1, s_k1_hi)
                    for slot, g in due(i, t, s):
                        if 0 <= slot - TURN < H:
                            h = slot - TURN
                            act.wait_ge(s_scores_t, g.count(H, h + 1))
                            nc.scalar.activation(probs[:, h % 3], bank_t[h % 2][:, :], ACT.Exp, scale=-1.0)\
                                .then_inc(s_probs, 1)
                    for slot, g in due(i, t, s):
                        if slot == C_COLS:
                            act.wait_ge(s_cols_ps, g.count())
                            nc.scalar.activation(c_cols[:, :, :], tiles(bank_b), ACT.Copy).then_inc(s_c_cols, 1)
                        if slot == XT2:
                            act.wait_ge(s_xt_ps[2], g.count())
                            relu_hi(2, bank_g)
                        if slot == H2:
                            act.wait_ge(s_h2_ps, g.count())
                            nc.scalar.activation(h2[:, :, :], tiles(bank_g), ACT.Copy).then_inc(s_h2, 1)
                        if slot == XT3:
                            act.wait_ge(s_xt_ps[3], g.count())
                            relu_hi(3, bank_g)
                        if slot == EDGE:
                            act.wait_ge(s_e_bias, g.count())
                            for r in range(NT):
                                nc.scalar.activation(e_pos[:, r, :], bank_g[:, 0:N], ACT.Exp, bias=e_bias[:, r, 0:1])
                                last = nc.scalar.activation(e_leak[:, r, :], bank_g[:, 0:N], ACT.Exp,
                                                            bias=e_bias[:, r, 1:2], scale=0.2)
                            last.then_inc(s_e, 1)
                        if slot == XW2:
                            act.wait_ge(s_xw2_ps, g.count())
                            nc.scalar.activation(xw2[:, :, :], tiles(bank_g), ACT.Copy).then_inc(s_xw2, 1)
                        if slot == XW1:
                            act.wait_ge(s_xw1_ps, g.count())
                            nc.scalar.activation(xw1[:, :, :], tiles(bank_g), ACT.Copy).then_inc(s_xw1, 1)
                        if slot == XW0:
                            act.wait_ge(s_xw0_ps, g.count())
                            nc.scalar.activation(xw0[:, :, :], tiles(bank_g), ACT.Copy).then_inc(s_xw0, 1)

            for t in range(AHEAD):
                iteration(0, t)
            with act.Fori(0, ROUNDS) as i:
                for u in range(BODY):
                    iteration(i, AHEAD + u)
            for t in range(ALL - BEHIND, ALL):
                iteration(0, t)

        @block.vector
        def _(dve):
            made = [0]

            def then(ins):
                made[0] += 1
                ins.then_inc(s_made, 1)
                dve.wait_ge(s_made, made[0])

            nc.vector.memset(ones[:, :], 1.0)
            nc.vector.memset(qk0[:, :, 2 * Q0:2 * Q0 + 1], 1.0)
            for n in range(2):
                nc.vector.memset(v_heads[:, n, :, :, HD:HE], 1.0)
            dve.wait_ge(s_weights, 16 * (len(wide) + 1))
            for n, (name, width) in enumerate(wide.items()):
                src = heads[:, n, 0:KT * width].rearrange("p (k n) -> p k n", k=KT)
                then(nc.vector.tensor_copy(w_hl[name][:, 0], src))
                nc.vector.tensor_tensor(w_hl[name][:, 1], src, w_hl[name][:, 0].bitcast(F32), ALU.subtract)
            dve.wait_ge(s_rows, 16 * (9 + HOPS))
            for k in range(KT):
                for n in range(2):
                    then(nc.vector.tensor_tensor_reduce(alpha[:, 0, :], e_pos[:, k, :], e_leak[:, n, :], 1.0, 0.0,
                                                        ALU.mult, ALU.add, a_part[:, 2 * k + n:2 * k + n + 1]))
            for n in range(2):
                then(nc.vector.tensor_tensor_reduce(alpha[:, 0, :], e_max[:, 0, :], e_leak[:, n, :], 1.0, 0.0,
                                                    ALU.mult, ALU.add, a_part[:, 4 + n:5 + n]))
            for k in range(KT):
                then(nc.vector.tensor_scalar(alpha[:, 0, 0:P], ones[:, :], a_part[:, 2 * k + 1:2 * k + 2], None, ALU.mult))
                then(nc.vector.tensor_copy(si_hl[:, 0, k, :], alpha[:, 0, 0:P]))
                then(nc.vector.tensor_tensor(si_hl[:, 1, k, :], alpha[:, 0, 0:P], si_hl[:, 0, k, :].bitcast(F32), ALU.subtract))
                for n, share in enumerate((1.0, 0.2)):
                    then(nc.vector.tensor_scalar(alpha[:, 1, n:n + 1], a_part[:, 2 * k:2 * k + 1], share, None, ALU.mult))
                then(nc.vector.tensor_copy(sj_hl[:, 0, k, :], alpha[:, 1, 0:2]))
                then(nc.vector.tensor_tensor(sj_hl[:, 1, k, :], alpha[:, 1, 0:2], sj_hl[:, 0, k, :].bitcast(F32), ALU.subtract))
            then(nc.vector.tensor_tensor(a_part[:, 6:7], a_part[:, 4:5], a_part[:, 5:6], ALU.add))
            for r in range(NT):
                then(nc.vector.tensor_tensor(e_const[:, r, 0:1], a_part[:, 6:7], a_part[:, 7:8], ALU.add))
                then(nc.vector.tensor_scalar(e_const[:, r, 1:2], e_const[:, r, 0:1], 0.2, None, ALU.mult))
            then(nc.vector.tensor_tensor(bk_row[:, :], hid_rows[0], hid_rows[1], ALU.add))
            for n in range(2, HOPS):
                then(nc.vector.tensor_tensor(bk_row[:, :], bk_row[:, :], hid_rows[n], ALU.add))
            dve.wait_ge(s_ident, 2)
            dve.drain().then_inc(s_setup, 1)

            def stat(n, src):
                for r in range(NT):
                    nc.vector.bn_stats(stats[n][:, r, :], src[:, r, :]).then_inc(s_stats[n], 1)

            def moment(n):
                for r in range(NT):
                    last = nc.vector.bn_aggr(moments[n][:, r, :], stats[n][:, r, :])
                last.then_inc(s_moments[n], 1)

            def relu_lo(n, src):
                hl = xt_hl[n // 2]
                nc.vector.scalar_tensor_tensor(out=flat(hl[:, 1]), in0=src[:, :], scalar=0.0, in1=flat(hl[:, 0]).bitcast(F32),
                                               op0=ALU.max, op1=ALU.subtract).then_inc(s_xt[n], 1)

            def bias_lo(hl, col, done):
                for k in range(KT):
                    last = nc.vector.scalar_tensor_tensor(
                        out=hl[:, 1, k, :], in0=tiles(bank_a)[:, k], scalar=bqk_col[:, col, k:k + 1],
                        in1=hl[:, 0, k, :].bitcast(F32), op0=ALU.add, op1=ALU.subtract)
                last.then_inc(done, 1)

            def scaled_add(dst, src, scale, more, done):
                for r in range(NT):
                    last = nc.vector.scalar_tensor_tensor(out=dst[:, r, :], in0=src[:, r, :], scalar=scale[:, r:r + 1],
                                                          in1=more[:, r, :], op0=ALU.mult, op1=ALU.add)
                last.then_inc(done, 1)

            def mask(g, h):
                for r in range(NT):
                    last = nc.vector.tensor_tensor_reduce(
                        masked[:, h % 3, r * N:(r + 1) * N], tiles(bank_s[h % 2])[:, r], adj_n[:, g.four, r, :],
                        SCALE1, LEAST, ALU.mult, ALU.max, s_top[:, h % 3, r:r + 1])
                last.then_inc(s_masked, 1)

            def iteration(i, t):
                for s in range(SLOTS):
                    for slot, g in due(i, t, s):
                        if 0 <= slot - HEAD < H:
                            h = slot - HEAD
                            dve.wait_ge(s_scores, g.count(H, h + 1))
                            settled(dve)
                            mask(g, h)
                    for slot, g in due(i, t, s):
                        if slot == NORM0:
                            dve.wait_ge(s_x[g.two], g.round(2, 16))
                            stat(0, x0[:, g.two])
                            dve.wait_ge(s_stats[0], g.count(NT, NT))
                            settled(dve)
                            moment(0)
                        if slot == XT0:
                            dve.wait_ge(s_xt_hi[0], g.count())
                            relu_lo(0, bank_a)
                        if slot == QK0:
                            dve.wait_ge(s_qk0_ps, g.count())
                            nc.vector.tensor_copy(qk0[:, :, 0:2 * Q0], qk0_ps).then_inc(s_qk0, 1)
                        if slot == EDGE_SUM:
                            dve.wait_ge(s_ak_ps, g.count())
                            settled(dve)
                            for r in range(NT):
                                nc.vector.tensor_tensor_reduce(qak[:, r, :], ak_ps[:, r, 0:Q0], qk0[:, r, 0:Q0], 1.0, 0.0,
                                                               ALU.mult, ALU.add, w_col[:, r:r + 1])
                            nc.vector.reciprocal(near_inv[:, g.four, :], ak_ps[:, :, Q0]).then_inc(s_w_col, 1)
                        if slot == W_ALL:
                            dve.wait_ge(s_w_ps, g.count())
                            nc.vector.tensor_reduce(w_neg[:, 0:1], bank_a[:, 0:N], AX_X, ALU.max, negate=True)\
                                .then_inc(s_w_max, 1)
                            dve.wait_ge(s_w_max, g.count())
                            nc.vector.tensor_scalar(w_neg[:, 1:2], w_neg[:, 0:1], SCALE0, None, ALU.mult).then_inc(s_w_neg, 1)
                        if slot == W_PROB:
                            dve.wait_ge(s_w_exp, g.count())
                            nc.vector.reciprocal(w_sum[:, 1:2], w_sum[:, 0:1]).then_inc(s_w_inv, 1)
                            dve.wait_ge(s_w_inv, g.count())
                            nc.vector.tensor_scalar(w_prob[:, :], w_e[:, :], w_sum[:, 1:2], None, ALU.mult).then_inc(s_w_prob, 1)
                        if slot == V0:
                            dve.wait_ge(s_v0_ps, g.count())
                            dve.wait_ge(s_w_prob, g.count())
                            scaled_add(x1, tiles(bank_a), w_prob, x0[:, g.two], s_x1)
                            dve.wait_ge(s_x1, g.count())
                            stat(1, x1)
                            dve.wait_ge(s_stats[1], g.count(NT, NT))
                            settled(dve)
                            moment(1)
                        if slot == XT1:
                            dve.wait_ge(s_xt_hi[1], g.count())
                            relu_lo(1, bank_a)
                        if slot == Q1:
                            dve.wait_ge(s_q1_hi, g.count())
                            bias_lo(q_hl, 0, s_q1)
                        if slot == K1:
                            dve.wait_ge(s_k1_hi, g.count())
                            bias_lo(k_hl, 1, s_k1)
                        if slot == V1:
                            dve.wait_ge(s_v1_ps, g.count())
                            for r in range(NT):
                                last = nc.vector.tensor_tensor(
                                    v_heads[:, g.two, r, :, 0:HD], tiles(bank_a)[:, r].rearrange("p (h e) -> p h e", h=H),
                                    bv_row[:, :].rearrange("p (h e) -> p h e", h=H), ALU.add)
                            last.then_inc(s_v1, 1)
                    for slot, g in due(i, t, s):
                        if slot == X2:
                            dve.wait_ge(s_x2_ps, g.count())
                            dve.wait_ge(s_x1_bias, g.count())
                            nc.vector.tensor_tensor(x2[:, :, :], tiles(bank_b), x1_bias[:, g.four], ALU.add).then_inc(s_x2, 1)
                            dve.wait_ge(s_x2, g.count())
                            stat(2, x2)
                            dve.wait_ge(s_stats[2], g.count(NT, NT))
                            settled(dve)
                            moment(2)
                        if slot == XT2:
                            dve.wait_ge(s_xt_hi[2], g.count())
                            relu_lo(2, bank_g)
                        if slot == NEAR:
                            dve.wait_ge(s_ah_ps, g.count())
                            dve.wait_ge(s_x2_bias, g.count())
                            scaled_add(x3, tiles(bank_g), near_inv[:, g.four], x2_bias, s_x3)
                            dve.wait_ge(s_x3, g.count())
                            stat(3, x3)
                            dve.wait_ge(s_stats[3], g.count(NT, NT))
                            settled(dve)
                            moment(3)
                        if slot == XT3:
                            dve.wait_ge(s_xt_hi[3], g.count())
                            relu_lo(3, bank_g)
                        if slot == EDGE:
                            dve.wait_ge(s_e_ps, g.count())
                            nc.vector.tensor_tensor(e_bias[:, :, :], bank_g[:, N:N + 2 * NT].rearrange("p (t n) -> p t n", t=NT),
                                                    e_const[:, :, :], ALU.add).then_inc(s_e_bias, 1)
                        if slot == ALPHA:
                            dve.wait_ge(s_e, g.count())
                            nc.vector.tensor_tensor(e_max, e_pos, e_leak, ALU.max).then_inc(s_e_max, 1)
                        if slot == XW1:
                            dve.wait_ge(s_a_ps, g.count())
                            nc.vector.tensor_scalar(a_inv[:, 0, :], bank_b[:, 0:NT], 1e-12, None, ALU.add).then_inc(s_a_sum, 1)
                            dve.wait_ge(s_a_sum, g.count())
                            nc.vector.reciprocal(a_inv[:, 1, :], a_inv[:, 0, :]).then_inc(s_a_inv, 1)
                        if slot == HOP1:
                            dve.wait_ge(s_y2_ps, g.count())
                            dve.wait_ge(s_xw1, g.count())
                            dve.wait_ge(s_a_inv, g.count())
                            scaled_add(y1, tiles(bank_g), a_inv[:, 1], xw1, s_y1)
                        if slot == HOP2:
                            dve.wait_ge(s_hop_ps, g.count())
                            dve.wait_ge(s_xw0_bias, g.count())
                            scaled_add(hid, tiles(bank_g), a_inv[:, 1], xw0_bias, s_hid)
                            dve.wait_ge(s_hid, g.count())
                            if not g.first:
                                dve.wait_ge(s_stored, g.before().count(16, 16))
                            nc.vector.scalar_tensor_tensor(out=flat(x_out[:, :, :]), in0=flat(hid[:, :, :]), scalar=0.0,
                                                           in1=flat(x3[:, :, :]), op0=ALU.max, op1=ALU.add).then_inc(s_out, 1)
                    for slot, g in due(i, t, s):
                        if slot - CONTEXT in (HG - 1, H - 1):
                            part = (slot - CONTEXT) // HG
                            dve.wait_ge(s_context, g.count(H, (part + 1) * HG))
                            at = slice(part * HG, (part + 1) * HG)
                            nc.vector.reciprocal(c_inv[:, :, at], ctx_ps[:, :, :, HD]).then_inc(s_c_inv, 1)
                            dve.wait_ge(s_c_inv, g.count(2, part + 1))
                            for r in range(NT):
                                last = nc.vector.tensor_tensor(
                                    c_rows[:, r, at, :], ctx_ps[:, r, :, 0:HD],
                                    c_inv[:, r, at].unsqueeze(2).broadcast_to([P, HG, HD]), ALU.mult)
                            last.then_inc(s_c_rows, 1)

            for t in range(AHEAD):
                iteration(0, t)
            with dve.Fori(0, ROUNDS) as i:
                for u in range(BODY):
                    iteration(i, AHEAD + u)
            for t in range(ALL - BEHIND, ALL):
                iteration(0, t)

        @block.tensor
        def _(pe):
            pe.wait_ge(s_setup, 1)

            def turn(dst, src):
                for k in range(2):
                    for r in range(2):
                        last = nc.tensor.transpose(dst[:, k * 256 + r * P:k * 256 + (r + 1) * P], src(r, k), ident[:, :])
                return last

            def split_product(dst, lhs, rhs):
                passes = [(k, p, q) for k in range(KT) for p, q in ((0, 0), (0, 1), (1, 0))]
                for n, (k, p, q) in enumerate(passes):
                    last = nc.tensor.matmul(dst, lhs(p, k), rhs(q, k), start=n == 0, stop=n == len(passes) - 1)
                return last

            def by_rows(dst, xt, name):
                w = w_hl[name]
                for r in range(NT):
                    last = split_product(dst[:, r], lambda p, k: xt[:, p, k, r * P:(r + 1) * P], lambda q, k: w[:, q, k, :])
                return last

            def by_cols(dst, xt, name):
                w = w_hl[name]
                for f in range(KT):
                    last = split_product(dst[:, f], lambda p, k: w[:, p, k, f * P:(f + 1) * P], lambda q, k: xt[:, q, k, :])
                return last

            def over_nodes(dst, lhs, rhs):
                for r in range(NT):
                    for k in range(NT):
                        last = nc.tensor.matmul(dst(r), lhs[:, k, r * P:(r + 1) * P], rhs(k), start=k == 0, stop=k == NT - 1)
                return last

            def norm_t(n, dst):
                turn(dst, lambda r, k: x_norm[n // 2][:, r, k * P:(k + 1) * P]).then_inc(s_xt_ps[n], 1)

            def scores(g, h):
                for r in range(NT):
                    last = nc.tensor.matmul(tiles(bank_s[h % 2])[:, r], q_stack[:, g.two, h, r * P:(r + 1) * P],
                                            k_stack[:, g.two, h, :], start=True, stop=True)
                last.then_inc(s_scores, 1)

            def context(g, h):
                for r in range(NT):
                    for k in range(NT):
                        last = nc.tensor.matmul(ctx_ps[:, r, h % HG, :], probs[:, h % 3, k * N + r * P:k * N + (r + 1) * P],
                                                v_heads[:, g.two, k, h, :], start=k == 0, stop=k == NT - 1)
                last.then_inc(s_context, 1)

            def iteration(i, t):
                xa, xc = xt_hl
                rows_a, rows_g, rows_b = tiles(bank_a), tiles(bank_g), tiles(bank_b)
                for s in range(SLOTS):
                    for slot, g in due(i, t, s):
                        if 0 <= slot - HEAD < H:
                            h = slot - HEAD
                            if h == 0:
                                pe.wait_ge(s_stack, g.count(STACK, STACK))
                            if not g.first or h > 1:
                                pe.wait_ge(s_masked, g.count(H, h - 1))
                            scores(g, h)
                    for slot, g in due(i, t, s):
                        if slot == XT0:
                            if not g.first:
                                pe.wait_ge(s_v1, g.before().count())
                            pe.wait_ge(s_norm[0], g.count())
                            norm_t(0, bank_a)
                        if slot == ADJ_T:
                            pe.wait_ge(s_adj[g.four], g.round(4, 16))
                            pe.wait_ge(s_xt[0], g.count())
                            turn(bank_a, lambda r, k: adj_n[:, g.four, r, k * P:(k + 1) * P]).then_inc(s_adj_ps, 1)
                        if slot == QK0:
                            pe.wait_ge(s_adj_t, g.count())
                            by_rows(qk0_ps, xa, "qk0").then_inc(s_qk0_ps, 1)
                        if slot == EDGE_SUM:
                            pe.wait_ge(s_qk0, g.count())
                            over_nodes(lambda r: ak_ps[:, r], adj_t[:, g.four],
                                       lambda k: qk0[:, k, Q0:2 * Q0 + 1]).then_inc(s_ak_ps, 1)
                        if slot == W_ALL:
                            pe.wait_ge(s_w_col, g.count())
                            for r in range(NT):
                                last = nc.tensor.matmul(bank_a[:, r * P:(r + 1) * P], w_col[:, r:r + 1].broadcast_to([P, P]),
                                                        ident[:, :], start=True, stop=True)
                            last.then_inc(s_w_ps, 1)
                        if slot == V0:
                            pe.wait_ge(s_w_exp, g.count())
                            by_rows(rows_a, xa, "v0").then_inc(s_v0_ps, 1)
                        if slot == XT1:
                            pe.wait_ge(s_x1, g.count())
                            pe.wait_ge(s_norm[1], g.count())
                            norm_t(1, bank_a)
                        if slot == Q1:
                            pe.wait_ge(s_xt[1], g.count())
                            by_cols(rows_a, xa, "q1").then_inc(s_q1_ps, 1)
                        if slot == K1:
                            pe.wait_ge(s_q1, g.count())
                            by_cols(rows_a, xa, "k1").then_inc(s_k1_ps, 1)
                        if slot == V1:
                            pe.wait_ge(s_k1, g.count())
                            by_rows(rows_a, xa, "v1").then_inc(s_v1_ps, 1)
                    for slot, g in due(i, t, s):
                        if 0 <= slot - TURN < H:
                            h = slot - TURN
                            pe.wait_ge(s_centred, g.count(H, h + 1))
                            if not g.first or h > 1:
                                pe.wait_ge(s_probs, g.count(H, h - 1))
                            turn(bank_t[h % 2], lambda r, k: centred[:, h % 3, r * N + k * P:r * N + (k + 1) * P])\
                                .then_inc(s_scores_t, 1)
                    for slot, g in due(i, t, s):
                        if slot == C_COLS:
                            pe.wait_ge(s_c_rows, g.count(2, 2))
                            if not g.first:
                                pe.wait_ge(s_a_inv, g.before().count())
                            turn(bank_b, lambda r, k: c_rows[:, r, k * HG:(k + 1) * HG, :].rearrange("p h e -> p (h e)"))\
                                .then_inc(s_cols_ps, 1)
                        if slot == X2:
                            pe.wait_ge(s_c_cols, g.count())
                            for r in range(NT):
                                for k in range(KT):
                                    last = nc.tensor.matmul(rows_b[:, r], c_cols[:, k, r * P:(r + 1) * P], wo_sb[:, k, :],
                                                            start=k == 0, stop=k == KT - 1)
                            last.then_inc(s_x2_ps, 1)
                        if slot == XT2:
                            if not g.first:
                                pe.wait_ge(s_hid, g.before().count())
                            pe.wait_ge(s_norm[2], g.count())
                            norm_t(2, bank_g)
                        if slot == H2:
                            pe.wait_ge(s_xt[2], g.count())
                            by_rows(rows_g, xc, "n2").then_inc(s_h2_ps, 1)
                        if slot == NEAR:
                            pe.wait_ge(s_h2, g.count())
                            over_nodes(lambda r: rows_g[:, r], adj_t[:, g.four], lambda k: h2[:, k, :]).then_inc(s_ah_ps, 1)
                        if slot == XT3:
                            pe.wait_ge(s_x3, g.count())
                            pe.wait_ge(s_norm[3], g.count())
                            norm_t(3, bank_g)
                        if slot == EDGE:
                            pe.wait_ge(s_xt[3], g.count())
                            split_product(bank_g[:, 0:N], lambda p, k: si_hl[:, p, k, :], lambda q, k: xc[:, q, k, :])
                            for r in range(NT):
                                last = split_product(bank_g[:, N + 2 * r:N + 2 * r + 2],
                                                     lambda p, k: xc[:, p, k, r * P:(r + 1) * P],
                                                     lambda q, k: sj_hl[:, q, k, :])
                            last.then_inc(s_e_ps, 1)
                        if slot == XW2:
                            pe.wait_ge(s_e, g.count())
                            by_rows(rows_g, xc, "h2").then_inc(s_xw2_ps, 1)
                        if slot == XW1:
                            pe.wait_ge(s_xw2, g.count())
                            by_rows(rows_g, xc, "h1").then_inc(s_xw1_ps, 1)
                            pe.wait_ge(s_alpha, g.count())
                            pe.wait_ge(s_x2, g.count())
                            over_nodes(lambda r: bank_b[:, r:r + 1], alpha, lambda k: ones[:, 0:1]).then_inc(s_a_ps, 1)
                        if slot == HOP1:
                            pe.wait_ge(s_xw1, g.count())
                            over_nodes(lambda r: rows_g[:, r], alpha, lambda k: xw2[:, k, :]).then_inc(s_y2_ps, 1)
                        if slot == XW0:
                            pe.wait_ge(s_y1, g.count())
                            by_rows(rows_g, xc, "h0").then_inc(s_xw0_ps, 1)
                        if slot == HOP2:
                            pe.wait_ge(s_xw0, g.count())
                            over_nodes(lambda r: rows_g[:, r], alpha, lambda k: y1[:, k, :]).then_inc(s_hop_ps, 1)
                    for slot, g in due(i, t, s):
                        if 0 <= slot - CONTEXT < H:
                            h = slot - CONTEXT
                            pe.wait_ge(s_probs, g.count(H, h + 1))
                            if h == 0:
                                pe.wait_ge(s_v1, g.count())
                            if h == HG or h == 0 and not g.first:
                                pe.wait_ge(s_c_rows, g.count(2, h // HG))
                            context(g, h)

            for t in range(AHEAD):
                iteration(0, t)
            with pe.Fori(0, ROUNDS) as i:
                for u in range(BODY):
                    iteration(i, AHEAD + u)
            for t in range(ALL - BEHIND, ALL):
                iteration(0, t)


_OUT = (32, 256, 256)


def kernel(**inputs):
    import numpy as _np
    import concourse.bacc as _bacc
    from concourse import mybir as _mybir
    from concourse.bass_utils import run_bass_kernel_spmd as _run

    turned = {"L0_gnn_W_qk", "L0_gnn_W_v", "L1_gnn_Wq", "L1_gnn_Wk", "L1_gnn_Wv", "L1_gnn_Wo"}
    order = ["x", "adj", "L0_gnn_W_qk", "L0_gnn_W_v", "L1_gnn_Wq", "L1_gnn_bq", "L1_gnn_Wk", "L1_gnn_bk",
             "L1_gnn_Wv", "L1_gnn_bv", "L1_gnn_Wo", "L1_gnn_bo", "L2_gnn_W", "L2_gnn_b", "L3_gnn_Wv",
             "L3_gnn_bv", "L3_gnn_aw", "L3_gnn_ab", "L3_gnn_Wk", "L3_gnn_bk"]
    nc = _bacc.Bacc("TRN2", target_bir_lowering=False, num_devices=1)
    arrays, args = {}, []
    for name in order:
        a = _np.asarray(inputs[name])
        a = _np.ascontiguousarray(a.T if name in turned else a)
        arrays[f"in_{name}"] = a
        args.append(nc.dram_tensor(f"in_{name}", a.shape, _mybir.dt.from_np(a.dtype), kind="ExternalInput").ap())
    args.append(nc.dram_tensor("out_x", _OUT, _mybir.dt.float32, kind="ExternalOutput").ap())
    graph_layers_kernel(nc, *args)
    r = _run(nc, [arrays], core_ids=[0])
    return r.results[0]["out_x"]
```

```python
from contextlib import ExitStack

import concourse.bass as bass
from concourse import mybir

F32 = mybir.dt.float32
F32R = mybir.dt.float32r
ALU = mybir.AluOpType
ACT = mybir.ActivationFunctionType
AX_X = mybir.AxisListType.X

P = 128
BODY = 4
SLOTS = 128
DEPTH = 4
LEAST = -3.0e38

SLOT = {
    "load": 0, "moments0": 6, "rstd0": 11, "norm0": 16, "turn0": 17, "xt0_hi": 22, "xt0_lo": 24,
    "adj_turn": 25, "adj_t": 31, "qk0_mm": 35, "qk0": 41, "near_k_mm": 45, "w_own": 54, "w_all_mm":
    58, "w_max": 61, "w_exp": 67, "w_prob": 72, "v0_mm": 73, "x1": 86, "x1_bias": 128, "rstd1": 90,
    "norm1": 92, "turn1": 103, "xt1_hi": 105, "xt1_lo": 108, "q1_mm": 112, "q1_hi": 120, "q1_lo":
    122, "k1_mm": 127, "k1_hi": 130, "k1_lo": 133, "v1_mm": 134, "v1": 141, "q_stack": 139,
    "k_stack": 162, "scores_mm": 211, "masked": 220, "centred": 224, "scores_turn": 231, "probs":
    237, "context_mm": 241, "c_rows_first": 304, "c_rows_last": 355, "c_turn": 361, "c_cols": 362,
    "x2_mm": 364, "x2": 366, "x2_bias": 387, "rstd2": 373, "norm2": 377, "turn2": 378, "xt2_hi":
    381, "xt2_lo": 384, "h2_mm": 385, "h2": 387, "x3_mm": 390, "x3": 402, "rstd3": 405, "norm3":
    411, "turn3": 416, "xt3_hi": 417, "xt3_lo": 423, "edge_mm": 424, "e_bias": 434, "edge_exp": 436,
    "e_max": 448, "alpha": 454, "xw2_mm": 442, "xw2": 452, "xw1_mm": 459, "xw1": 466, "a_sum_mm":
    462, "a_inv": 478, "y1_mm": 471, "y1": 481, "xw0_mm": 490, "xw0": 491, "xw0_bias": 497,
    "hid_mm": 492, "x_out": 498, "store": 502,
}
HEAD_STEP = SLOTS // 8


class Graph:

    def __init__(self, i, c):
        self.i, self.c = i, c
        self.two, self.four = c % 2, c % 4
        self.first = isinstance(i, int) and c == 0

    def number(self):
        return BODY * self.i + self.c

    def count(self, each=1, events=1):
        return BODY * each * self.i + (each * self.c + events)

    def round(self, ring, each):
        return each * (BODY // ring) * self.i + each * (self.c // ring + 1)

    def before(self, n=1):
        return Graph(self.i, self.c - n)


def graph_layers_kernel(nc, x, adj, w_qk0, w_v0, w_q1, b_q1, w_k1, b_k1, w_v1, b_v1, w_o1, b_o1,
                        w2, b2, w_v3, b_v3, a_w3, a_b3, w_k3, b_k3, out):
    G, N, D = x.shape
    NT, KT = N // P, D // P
    Q0 = w_qk0.shape[1] // 2
    H = 8
    HD = D // H
    HE = HD + 1
    HG = P // HD
    HOPS = w_k3.shape[0]
    SCALE0 = float(Q0) ** -0.5
    SCALE1 = 2.0 * float(HD) ** -0.5
    ALL = G + DEPTH - 1
    AHEAD, BEHIND = DEPTH, DEPTH - 1
    ROUNDS = (ALL - AHEAD - BEHIND) // BODY
    assert (ALL - AHEAD - BEHIND) % BODY == 0 and NT == 2 and KT == 2

    with ExitStack() as ctx:
        def sb(name, shape, dt=F32):
            return ctx.enter_context(nc.sbuf_tensor(name, shape, dt))

        def bank(name):
            return ctx.enter_context(nc.psum_tensor(name, [P, 512], F32))

        def sem(name):
            return ctx.enter_context(nc.semaphore(name))

        x0 = sb("x0", [P, 2, NT, D])
        adj_n = sb("adj_n", [P, 4, NT, N])
        adj_t = sb("adj_t", [P, 4, NT, N])
        x1_bias = sb("x1_bias", [P, 4, NT, D])
        near_inv = sb("near_inv", [P, 4, NT])
        q_stack = sb("q_stack", [P, 2, H, N], F32R)
        k_stack = sb("k_stack", [P, 2, H, N], F32R)
        v_heads = sb("v_heads", [P, 2, NT, H, HE])
        x_out = sb("x_out", [P, NT, D])

        x1 = sb("x1", [P, NT, D])
        qk0 = sb("qk0", [P, NT, 2 * Q0 + 1])
        qak = sb("qak", [P, NT, Q0])
        w_col = sb("w_col", [P, NT])
        w_neg = sb("w_neg", [P, 2])
        w_exp = sb("w_exp", [P, N])
        w_sum = sb("w_sum", [P, 2])
        w_e = sb("w_e", [P, NT])
        w_prob = sb("w_prob", [P, NT])
        q_hl = sb("q_hl", [P, 2, KT, N], F32R)
        k_hl = sb("k_hl", [P, 2, KT, N], F32R)

        heads = sb("heads", [P, 9, NT * N])
        masked, centred, probs = heads[:, 0:3, :], heads[:, 3:6, :], heads[:, 6:9, :]
        s_top = sb("s_top", [P, 3, NT])
        c_inv = sb("c_inv", [P, NT, H])
        c_rows = sb("c_rows", [P, NT, H, HD])
        c_cols = sb("c_cols", [P, KT, N])
        x2 = sb("x2", [P, NT, D])
        x2_bias = sb("x2_bias", [P, NT, D])

        h2 = sb("h2", [P, NT, D])
        x3 = sb("x3", [P, NT, D])
        e_bias = sb("e_bias", [P, NT, 2])
        edges = sb("edges", [P, 4, NT, N])
        e_pos, e_leak, e_max, alpha = (edges[:, n] for n in range(4))
        a_inv = sb("a_inv", [P, 2, NT])
        xw2 = sb("xw2", [P, NT, D])
        xw1 = sb("xw1", [P, NT, D])
        xw0 = sb("xw0", [P, NT, D])
        xw0_bias = sb("xw0_bias", [P, NT, D])
        y1 = sb("y1", [P, NT, D])
        hid = sb("hid", [P, NT, D])

        x_norm = [sb(f"x_norm{n}", [P, NT, D]) for n in range(2)]
        xt_hl = [sb(f"xt_hl{n}", [P, 2, KT, N], F32R) for n in range(2)]
        stats = [sb(f"stats{n}", [P, NT, 6]) for n in range(4)]
        moments = [sb(f"moments{n}", [P, NT, 2]) for n in range(4)]
        var_eps = [sb(f"var_eps{n}", [P, NT]) for n in range(4)]
        rstd = [sb(f"rstd{n}", [P, NT]) for n in range(4)]

        wide = {"qk0": 2 * Q0, "v0": D, "q1": D, "k1": D, "v1": D, "n2": D, "h0": D, "h1": D, "h2": D}
        w_hl = {k: sb("w_" + k, [P, 2, KT, n], F32R) for k, n in wide.items()}
        w_src = {"qk0": w_qk0, "v0": w_v0, "q1": w_q1, "k1": w_k1, "v1": w_v1, "n2": w2,
                 "h0": w_k3[0], "h1": w_k3[1], "h2": w_k3[2]}
        wo_sb = sb("wo_sb", [P, KT, D])
        si_hl = sb("si_hl", [P, 2, KT, P], F32R)
        sj_hl = sb("sj_hl", [P, 2, KT, 2], F32R)
        bo_row = sb("bo_row", [P, D])
        bv_row = sb("bv_row", [P, D])
        b2_row = sb("b2_row", [P, D])
        bk_row = sb("bk_row", [P, D])
        bqk_col = sb("bqk_col", [P, 2, KT])
        e_const = sb("e_const", [P, NT, 2])
        a_part = sb("a_part", [P, 8])
        ident = sb("ident", [P, P])
        ones = sb("ones", [P, P])
        half = sb("half", [P, NT])

        bank_s = [bank("bank_s0"), bank("bank_s1")]
        bank_t = [bank("bank_t0"), bank("bank_t1")]
        bank_c = bank("bank_c")
        bank_a = bank("bank_a")
        bank_b = bank("bank_b")
        bank_g = bank("bank_g")
        ctx_ps = bank_c[:, 0:NT * HG * HE].rearrange("p (t h e) -> p t h e", t=NT, h=HG)

        def tiles(b):
            return b[:, :].rearrange("p (t n) -> p t n", t=2)

        s_weights = sem("s_weights")
        s_rows = sem("s_rows")
        s_made = sem("s_made")
        s_ident = sem("s_ident")
        s_setup = sem("s_setup")
        s_carry = sem("s_carry")
        s_x = [sem(f"s_x_in{n}") for n in range(2)]
        s_adj = [sem(f"s_adj_in{n}") for n in range(4)]
        s_stats = [sem(f"s_stats{n}") for n in range(4)]
        s_moments = [sem(f"s_moments{n}") for n in range(4)]
        s_mean = [sem(f"s_mean{n}") for n in range(4)]
        s_rstd = [sem(f"s_rstd{n}") for n in range(4)]
        s_norm = [sem(f"s_norm{n}") for n in range(4)]
        s_xt_ps = [sem(f"s_xt_ps{n}") for n in range(4)]
        s_xt_hi = [sem(f"s_xt_hi{n}") for n in range(4)]
        s_xt = [sem(f"s_xt{n}") for n in range(4)]
        s_adj_ps, s_adj_t = sem("s_adj_ps"), sem("s_adj_t")
        s_qk0_ps, s_qk0 = sem("s_qk0_ps"), sem("s_qk0")
        s_ak_ps, s_w_col = sem("s_ak_ps"), sem("s_w_col")
        s_w_max = sem("s_w_max")
        s_w_ps, s_w_neg, s_w_exp, s_w_inv, s_w_prob = (
            sem("s_w_ps"), sem("s_w_neg"), sem("s_w_exp"), sem("s_w_inv"), sem("s_w_prob"))
        s_v0_ps, s_x1, s_x1_bias = sem("s_v0_ps"), sem("s_x1"), sem("s_x1_bias")
        s_q1_ps, s_q1_hi, s_q1 = sem("s_q1_ps"), sem("s_q1_hi"), sem("s_q1")
        s_k1_ps, s_k1_hi, s_k1 = sem("s_k1_ps"), sem("s_k1_hi"), sem("s_k1")
        s_v1_ps, s_v1 = sem("s_v1_ps"), sem("s_v1")
        s_stack = sem("s_stack")
        s_scores, s_masked, s_centred, s_scores_t, s_probs, s_context = (
            sem("s_scores"), sem("s_masked"), sem("s_centred"), sem("s_scores_t"), sem("s_probs"),
            sem("s_context"))
        s_c_inv, s_c_rows, s_cols_ps, s_c_cols, s_x2_ps, s_x2, s_x2_bias = (
            sem("s_c_inv"), sem("s_c_rows"), sem("s_cols_ps"), sem("s_c_cols"), sem("s_x2_ps"),
            sem("s_x2"), sem("s_x2_bias"))
        s_h2_ps, s_h2, s_ah_ps, s_x3 = sem("s_h2_ps"), sem("s_h2"), sem("s_ah_ps"), sem("s_x3")
        s_e_ps, s_e_bias, s_e, s_e_max, s_alpha = (
            sem("s_e_ps"), sem("s_e_bias"), sem("s_e"), sem("s_e_max"), sem("s_alpha"))
        s_a_ps, s_a_sum, s_a_inv = sem("s_a_ps"), sem("s_a_sum"), sem("s_a_inv")
        s_xw2_ps, s_xw2, s_xw1_ps, s_xw1, s_xw0_ps, s_xw0, s_xw0_bias = (
            sem("s_xw2_ps"), sem("s_xw2"), sem("s_xw1_ps"), sem("s_xw1"), sem("s_xw0_ps"),
            sem("s_xw0"), sem("s_xw0_bias"))
        s_y2_ps, s_y1, s_hop_ps, s_hid, s_out = (
            sem("s_y2_ps"), sem("s_y1"), sem("s_hop_ps"), sem("s_hid"), sem("s_out"))
        s_stored = sem("s_stored")

        block = ctx.enter_context(nc.Block())

        def due(i, t, s):
            inside = not isinstance(i, int)
            return [(n * SLOTS + s, Graph(i, t - n)) for n in range(DEPTH) if inside or 0 <= t - n < G]

        def head_at(slot, step):
            h, off = divmod(slot - SLOT[step], HEAD_STEP)
            return h if off == 0 and 0 <= h < H else None

        def settled(eng):
            eng.sem_inc(s_carry, 1)

        def flat(ap):
            return ap.rearrange("p t n -> p (t n)")

        qk0_ps = bank_a[:, 0:NT * 2 * Q0].rearrange("p (t n) -> p t n", t=NT)
        ak_ps = bank_a[:, 0:NT * (Q0 + 1)].rearrange("p (t n) -> p t n", t=NT)
        hid_rows = [flat(hid[:, :, :])[:, 0:D], flat(hid[:, :, :])[:, D:2 * D], flat(y1[:, :, :])[:, 0:D]]
        STACK = 2 * HG * HG * 16

        @block.sync
        def _(sp):
            for name, src in w_src.items():
                n = list(wide).index(name)
                dst = heads[:, n, 0:KT * wide[name]].rearrange("p (k n) -> p k n", k=KT)
                sp.dma_start(dst, src.rearrange("(k p) n -> p k n", p=P)).then_inc(s_weights, 16)
            sp.dma_start(wo_sb[:, :, :], w_o1.rearrange("(k p) n -> p k n", p=P)).then_inc(s_weights, 16)
            sp.dma_start(e_pos, w_v3.rearrange("(k p) n -> p k n", p=P)).then_inc(s_rows, 16)
            sp.dma_start(e_leak, a_w3.rearrange("(o t n) u -> o t (n u)", o=1, t=2).broadcast_to([P, 2, D])).then_inc(s_rows, 16)
            sp.dma_start(e_max[:, 0], b_v3.rearrange("(o n) -> o n", o=1).broadcast_to([P, D])).then_inc(s_rows, 16)
            sp.dma_start(a_part[:, 7:8], a_b3.rearrange("(o n) -> o n", o=1).broadcast_to([P, 1])).then_inc(s_rows, 16)
            for row, src in ((bo_row, b_o1), (bv_row, b_v1), (b2_row, b2)):
                sp.dma_start(row[:, :], src.rearrange("(o n) -> o n", o=1).broadcast_to([P, D])).then_inc(s_rows, 16)
            for n in range(HOPS):
                sp.dma_start(hid_rows[n], b_k3[n:n + 1, :].broadcast_to([P, D])).then_inc(s_rows, 16)
            for n, src in enumerate((b_q1, b_k1)):
                sp.dma_start(bqk_col[:, n, :], src.rearrange("(k p) -> p k", p=P),
                             allow_slow_non_contiguous=True).then_inc(s_rows, 16)

            def load(g):
                if g.c >= 2:
                    sp.wait_ge(s_x1, g.before(2).count())
                    settled(sp)
                at = bass.ds(g.number(), 1)
                sp.dma_start(x0[:, g.two, :, :], x[at].rearrange("a (t p) d -> p (a t) d", p=P))\
                    .then_inc(s_x[g.two], 16)
                sp.dma_start(adj_n[:, g.four, :, :], adj[at].rearrange("a (t p) d -> p (a t) d", p=P))\
                    .then_inc(s_adj[g.four], 16)

            def stack(g, src, dst, order):
                for j in range(HG):
                    for c in range(HG):
                        sp.dma_start(
                            dst[c * HD:(c + 1) * HD, g.two, j::HG, :].bitcast(F32),
                            src[j * HD:(j + 1) * HD, order[c], :, :].bitcast(F32)).then_inc(s_stack, 16)

            def store(g):
                sp.wait_ge(s_out, g.count())
                settled(sp)
                at = bass.ds(g.number(), 1)
                sp.dma_start(out[at].rearrange("a (t p) d -> p (a t) d", p=P), x_out[:, :, :]).then_inc(s_stored, 16)

            def iteration(i, t):
                for s in range(SLOTS):
                    for slot, g in due(i, t, s):
                        if slot == SLOT["load"]:
                            load(g)
                        if slot == SLOT["q_stack"]:
                            sp.wait_ge(s_q1, g.count())
                            settled(sp)
                            stack(g, q_hl, q_stack, [0, 1, 0, 1])
                        if slot == SLOT["k_stack"]:
                            sp.wait_ge(s_k1, g.count())
                            settled(sp)
                            stack(g, k_hl, k_stack, [0, 0, 1, 1])
                        if slot == SLOT["store"]:
                            store(g)

            for t in range(AHEAD):
                iteration(0, t)
            with sp.Fori(0, ROUNDS) as i:
                for u in range(BODY):
                    iteration(i, AHEAD + u)
            for t in range(ALL - BEHIND, ALL):
                iteration(0, t)
            sp.wait_ge(s_stored, 16 * G)

        @block.gpsimd
        def _(pool):
            nc.gpsimd.memset(ident[:, :], 0.0).then_inc(s_ident, 1)
            nc.gpsimd.memset(half[:, :], -0.5)
            pool.wait_ge(s_ident, 1)
            nc.gpsimd.affine_select(out=ident[:, :], in_=ident[:, :], compare_op=ALU.not_equal, fill=1.0,
                                    base=0, pattern=[[-1, P]], channel_multiplier=1).then_inc(s_ident, 1)
            pool.wait_ge(s_setup, 1)

            def add_row(dst, src, row, done):
                for r in range(NT):
                    last = nc.gpsimd.tensor_tensor(dst[:, r, :], src[:, r, :], row[:, :], ALU.add)
                last.then_inc(done, 1)

            def centre(h):
                for r in range(NT):
                    at = slice(r * N, (r + 1) * N)
                    last = nc.gpsimd.tensor_scalar(centred[:, h % 3, at], masked[:, h % 3, at], -1.0,
                                                   s_top[:, h % 3, r:r + 1], ALU.mult, ALU.add)
                last.then_inc(s_centred, 1)

            def iteration(i, t):
                for s in range(SLOTS):
                    for slot, g in due(i, t, s):
                        if (h := head_at(slot, "centred")) is not None:
                            pool.wait_ge(s_masked, g.count(H, h + 1))
                            settled(pool)
                            centre(h)
                        for n in range(4):
                            if slot == SLOT[f"rstd{n}"]:
                                pool.wait_ge(s_moments[n], g.count())
                                nc.gpsimd.tensor_tensor(rstd[n][:, :], var_eps[n][:, :], half[:, :], ALU.pow)\
                                    .then_inc(s_rstd[n], 1)
                        if slot == SLOT["x1_bias"]:
                            pool.wait_ge(s_x1, g.count())
                            add_row(x1_bias[:, g.four], x1, bo_row, s_x1_bias)
                        if slot == SLOT["x2_bias"]:
                            pool.wait_ge(s_x2, g.count())
                            add_row(x2_bias, x2, b2_row, s_x2_bias)
                        if slot == SLOT["alpha"]:
                            pool.wait_ge(s_e_max, g.count())
                            nc.gpsimd.tensor_tensor(alpha, e_max, adj_t[:, g.four], ALU.mult).then_inc(s_alpha, 1)
                        if slot == SLOT["xw0_bias"]:
                            pool.wait_ge(s_xw0, g.count())
                            add_row(xw0_bias, xw0, bk_row, s_xw0_bias)

            for t in range(AHEAD):
                iteration(0, t)
            with pool.Fori(0, ROUNDS) as i:
                for u in range(BODY):
                    iteration(i, AHEAD + u)
            for t in range(ALL - BEHIND, ALL):
                iteration(0, t)

        @block.scalar
        def _(act):
            act.wait_ge(s_setup, 1)

            def relu_hi(n, src):
                nc.scalar.activation(flat(xt_hl[n // 2][:, 0]), src[:, :], ACT.Relu).then_inc(s_xt_hi[n], 1)

            def bias_hi(dst, col, done):
                for k in range(KT):
                    last = nc.scalar.activation(dst[:, 0, k, :], tiles(bank_a)[:, k], ACT.Identity,
                                                bias=bqk_col[:, col, k:k + 1])
                last.then_inc(done, 1)

            def iteration(i, t):
                for s in range(SLOTS):
                    for slot, g in due(i, t, s):
                        if slot == SLOT["xt0_hi"]:
                            act.wait_ge(s_xt_ps[0], g.count())
                            relu_hi(0, bank_a)
                        if slot == SLOT["adj_t"]:
                            act.wait_ge(s_adj_ps, g.count())
                            nc.scalar.activation(adj_t[:, g.four], tiles(bank_a), ACT.Copy).then_inc(s_adj_t, 1)
                        if slot == SLOT["w_exp"]:
                            act.wait_ge(s_w_neg, g.count())
                            nc.scalar.activation(w_exp[:, :], bank_a[:, 0:N], ACT.Exp, bias=w_neg[:, 1:2], scale=SCALE0,
                                                 accum_out=w_sum[:, 0:1])
                            nc.scalar.activation(w_e[:, :], w_col[:, :], ACT.Exp, bias=w_neg[:, 1:2], scale=SCALE0)\
                                .then_inc(s_w_exp, 1)
                        if slot == SLOT["xt1_hi"]:
                            act.wait_ge(s_xt_ps[1], g.count())
                            relu_hi(1, bank_a)
                        if slot == SLOT["q1_hi"]:
                            act.wait_ge(s_q1_ps, g.count())
                            if not g.first:
                                act.wait_ge(s_stack, g.before().count(STACK, STACK))
                            bias_hi(q_hl, 0, s_q1_hi)
                        if slot == SLOT["k1_hi"]:
                            act.wait_ge(s_k1_ps, g.count())
                            bias_hi(k_hl, 1, s_k1_hi)
                        if (h := head_at(slot, "probs")) is not None:
                            act.wait_ge(s_scores_t, g.count(H, h + 1))
                            nc.scalar.activation(probs[:, h % 3], bank_t[h % 2][:, :], ACT.Exp, scale=-1.0)\
                                .then_inc(s_probs, 1)
                        if slot == SLOT["c_cols"]:
                            act.wait_ge(s_cols_ps, g.count())
                            nc.scalar.activation(c_cols[:, :, :], tiles(bank_b), ACT.Copy).then_inc(s_c_cols, 1)
                        if slot == SLOT["xt2_hi"]:
                            act.wait_ge(s_xt_ps[2], g.count())
                            relu_hi(2, bank_g)
                        if slot == SLOT["h2"]:
                            act.wait_ge(s_h2_ps, g.count())
                            nc.scalar.activation(h2[:, :, :], tiles(bank_g), ACT.Copy).then_inc(s_h2, 1)
                        if slot == SLOT["xt3_hi"]:
                            act.wait_ge(s_xt_ps[3], g.count())
                            relu_hi(3, bank_g)
                        if slot == SLOT["edge_exp"]:
                            act.wait_ge(s_e_bias, g.count())
                            for r in range(NT):
                                nc.scalar.activation(e_pos[:, r, :], bank_g[:, 0:N], ACT.Exp, bias=e_bias[:, r, 0:1])
                                last = nc.scalar.activation(e_leak[:, r, :], bank_g[:, 0:N], ACT.Exp,
                                                            bias=e_bias[:, r, 1:2], scale=0.2)
                            last.then_inc(s_e, 1)
                        if slot == SLOT["xw2"]:
                            act.wait_ge(s_xw2_ps, g.count())
                            nc.scalar.activation(xw2[:, :, :], tiles(bank_g), ACT.Copy).then_inc(s_xw2, 1)
                        if slot == SLOT["xw1"]:
                            act.wait_ge(s_xw1_ps, g.count())
                            nc.scalar.activation(xw1[:, :, :], tiles(bank_g), ACT.Copy).then_inc(s_xw1, 1)
                        if slot == SLOT["xw0"]:
                            act.wait_ge(s_xw0_ps, g.count())
                            nc.scalar.activation(xw0[:, :, :], tiles(bank_g), ACT.Copy).then_inc(s_xw0, 1)

            for t in range(AHEAD):
                iteration(0, t)
            with act.Fori(0, ROUNDS) as i:
                for u in range(BODY):
                    iteration(i, AHEAD + u)
            for t in range(ALL - BEHIND, ALL):
                iteration(0, t)

        @block.vector
        def _(dve):
            made = [0]

            def then(ins):
                made[0] += 1
                ins.then_inc(s_made, 1)
                dve.wait_ge(s_made, made[0])

            nc.vector.memset(ones[:, :], 1.0)
            nc.vector.memset(qk0[:, :, 2 * Q0:2 * Q0 + 1], 1.0)
            for n in range(2):
                nc.vector.memset(v_heads[:, n, :, :, HD:HE], 1.0)
            dve.wait_ge(s_weights, 16 * (len(wide) + 1))
            for n, (name, width) in enumerate(wide.items()):
                src = heads[:, n, 0:KT * width].rearrange("p (k n) -> p k n", k=KT)
                then(nc.vector.tensor_copy(w_hl[name][:, 0], src))
                nc.vector.tensor_tensor(w_hl[name][:, 1], src, w_hl[name][:, 0].bitcast(F32), ALU.subtract)
            dve.wait_ge(s_rows, 16 * (9 + HOPS))
            for k in range(KT):
                for n in range(2):
                    then(nc.vector.tensor_tensor_reduce(alpha[:, 0, :], e_pos[:, k, :], e_leak[:, n, :], 1.0, 0.0,
                                                        ALU.mult, ALU.add, a_part[:, 2 * k + n:2 * k + n + 1]))
            for n in range(2):
                then(nc.vector.tensor_tensor_reduce(alpha[:, 0, :], e_max[:, 0, :], e_leak[:, n, :], 1.0, 0.0,
                                                    ALU.mult, ALU.add, a_part[:, 4 + n:5 + n]))
            for k in range(KT):
                then(nc.vector.tensor_scalar(alpha[:, 0, 0:P], ones[:, :], a_part[:, 2 * k + 1:2 * k + 2], None, ALU.mult))
                then(nc.vector.tensor_copy(si_hl[:, 0, k, :], alpha[:, 0, 0:P]))
                then(nc.vector.tensor_tensor(si_hl[:, 1, k, :], alpha[:, 0, 0:P], si_hl[:, 0, k, :].bitcast(F32), ALU.subtract))
                for n, share in enumerate((1.0, 0.2)):
                    then(nc.vector.tensor_scalar(alpha[:, 1, n:n + 1], a_part[:, 2 * k:2 * k + 1], share, None, ALU.mult))
                then(nc.vector.tensor_copy(sj_hl[:, 0, k, :], alpha[:, 1, 0:2]))
                then(nc.vector.tensor_tensor(sj_hl[:, 1, k, :], alpha[:, 1, 0:2], sj_hl[:, 0, k, :].bitcast(F32), ALU.subtract))
            then(nc.vector.tensor_tensor(a_part[:, 6:7], a_part[:, 4:5], a_part[:, 5:6], ALU.add))
            for r in range(NT):
                then(nc.vector.tensor_tensor(e_const[:, r, 0:1], a_part[:, 6:7], a_part[:, 7:8], ALU.add))
                then(nc.vector.tensor_scalar(e_const[:, r, 1:2], e_const[:, r, 0:1], 0.2, None, ALU.mult))
            then(nc.vector.tensor_tensor(bk_row[:, :], hid_rows[0], hid_rows[1], ALU.add))
            for n in range(2, HOPS):
                then(nc.vector.tensor_tensor(bk_row[:, :], bk_row[:, :], hid_rows[n], ALU.add))
            dve.wait_ge(s_ident, 2)
            dve.drain().then_inc(s_setup, 1)

            def stat(n, src):
                for r in range(NT):
                    nc.vector.bn_stats(stats[n][:, r, :], src[:, r, :]).then_inc(s_stats[n], 1)

            def moment(n):
                for r in range(NT):
                    last = nc.vector.bn_aggr(moments[n][:, r, :], stats[n][:, r, :])
                last.then_inc(s_mean[n], 1)

            def normalise(n, src):
                for r in range(NT):
                    last = nc.vector.tensor_scalar(x_norm[n // 2][:, r, :], src[:, r, :], moments[n][:, r, 0:1],
                                                   rstd[n][:, r:r + 1], ALU.subtract, ALU.mult)
                last.then_inc(s_norm[n], 1)

            def relu_lo(n, src):
                hl = xt_hl[n // 2]
                nc.vector.scalar_tensor_tensor(out=flat(hl[:, 1]), in0=src[:, :], scalar=0.0, in1=flat(hl[:, 0]).bitcast(F32),
                                               op0=ALU.max, op1=ALU.subtract).then_inc(s_xt[n], 1)

            def bias_lo(hl, col, done):
                for k in range(KT):
                    last = nc.vector.scalar_tensor_tensor(
                        out=hl[:, 1, k, :], in0=tiles(bank_a)[:, k], scalar=bqk_col[:, col, k:k + 1],
                        in1=hl[:, 0, k, :].bitcast(F32), op0=ALU.add, op1=ALU.subtract)
                last.then_inc(done, 1)

            def scaled_add(dst, src, scale, more, done):
                for r in range(NT):
                    last = nc.vector.scalar_tensor_tensor(out=dst[:, r, :], in0=src[:, r, :], scalar=scale[:, r:r + 1],
                                                          in1=more[:, r, :], op0=ALU.mult, op1=ALU.add)
                last.then_inc(done, 1)

            def mask(g, h):
                for r in range(NT):
                    last = nc.vector.tensor_tensor_reduce(
                        masked[:, h % 3, r * N:(r + 1) * N], tiles(bank_s[h % 2])[:, r], adj_n[:, g.four, r, :],
                        SCALE1, LEAST, ALU.mult, ALU.max, s_top[:, h % 3, r:r + 1])
                last.then_inc(s_masked, 1)

            def iteration(i, t):
                for s in range(SLOTS):
                    for slot, g in due(i, t, s):
                        if (h := head_at(slot, "masked")) is not None:
                            dve.wait_ge(s_scores, g.count(H, h + 1))
                            settled(dve)
                            mask(g, h)
                        if slot == SLOT["moments0"]:
                            dve.wait_ge(s_x[g.two], g.round(2, 16))
                            stat(0, x0[:, g.two])
                            dve.wait_ge(s_stats[0], g.count(NT, NT))
                            settled(dve)
                            moment(0)
                            dve.wait_ge(s_mean[0], g.count())
                            nc.vector.tensor_scalar(var_eps[0][:, :], moments[0][:, :, 1], 1e-5, None, ALU.add)\
                                .then_inc(s_moments[0], 1)
                        if slot == SLOT["norm0"]:
                            dve.wait_ge(s_rstd[0], g.count())
                            normalise(0, x0[:, g.two])
                        if slot == SLOT["xt0_lo"]:
                            dve.wait_ge(s_xt_hi[0], g.count())
                            relu_lo(0, bank_a)
                        if slot == SLOT["qk0"]:
                            dve.wait_ge(s_qk0_ps, g.count())
                            nc.vector.tensor_copy(qk0[:, :, 0:2 * Q0], qk0_ps).then_inc(s_qk0, 1)
                        if slot == SLOT["w_own"]:
                            dve.wait_ge(s_ak_ps, g.count())
                            settled(dve)
                            for r in range(NT):
                                nc.vector.tensor_tensor_reduce(qak[:, r, :], ak_ps[:, r, 0:Q0], qk0[:, r, 0:Q0], 1.0, 0.0,
                                                               ALU.mult, ALU.add, w_col[:, r:r + 1])
                            nc.vector.reciprocal(near_inv[:, g.four, :], ak_ps[:, :, Q0]).then_inc(s_w_col, 1)
                        if slot == SLOT["w_max"]:
                            dve.wait_ge(s_w_ps, g.count())
                            nc.vector.tensor_reduce(w_neg[:, 0:1], bank_a[:, 0:N], AX_X, ALU.max, negate=True)\
                                .then_inc(s_w_max, 1)
                            dve.wait_ge(s_w_max, g.count())
                            nc.vector.tensor_scalar(w_neg[:, 1:2], w_neg[:, 0:1], SCALE0, None, ALU.mult).then_inc(s_w_neg, 1)
                        if slot == SLOT["w_prob"]:
                            dve.wait_ge(s_w_exp, g.count())
                            nc.vector.reciprocal(w_sum[:, 1:2], w_sum[:, 0:1]).then_inc(s_w_inv, 1)
                            dve.wait_ge(s_w_inv, g.count())
                            nc.vector.tensor_scalar(w_prob[:, :], w_e[:, :], w_sum[:, 1:2], None, ALU.mult).then_inc(s_w_prob, 1)
                        if slot == SLOT["x1"]:
                            dve.wait_ge(s_v0_ps, g.count())
                            dve.wait_ge(s_w_prob, g.count())
                            scaled_add(x1, tiles(bank_a), w_prob, x0[:, g.two], s_x1)
                            dve.wait_ge(s_x1, g.count())
                            stat(1, x1)
                            dve.wait_ge(s_stats[1], g.count(NT, NT))
                            settled(dve)
                            moment(1)
                            dve.wait_ge(s_mean[1], g.count())
                            nc.vector.tensor_scalar(var_eps[1][:, :], moments[1][:, :, 1], 1e-5, None, ALU.add)\
                                .then_inc(s_moments[1], 1)
                        if slot == SLOT["norm1"]:
                            dve.wait_ge(s_rstd[1], g.count())
                            normalise(1, x1)
                        if slot == SLOT["xt1_lo"]:
                            dve.wait_ge(s_xt_hi[1], g.count())
                            relu_lo(1, bank_a)
                        if slot == SLOT["q1_lo"]:
                            dve.wait_ge(s_q1_hi, g.count())
                            bias_lo(q_hl, 0, s_q1)
                        if slot == SLOT["k1_lo"]:
                            dve.wait_ge(s_k1_hi, g.count())
                            bias_lo(k_hl, 1, s_k1)
                        if slot == SLOT["v1"]:
                            dve.wait_ge(s_v1_ps, g.count())
                            for r in range(NT):
                                last = nc.vector.tensor_tensor(
                                    v_heads[:, g.two, r, :, 0:HD], tiles(bank_a)[:, r].rearrange("p (h e) -> p h e", h=H),
                                    bv_row[:, :].rearrange("p (h e) -> p h e", h=H), ALU.add)
                            last.then_inc(s_v1, 1)
                        if slot == SLOT["x2"]:
                            dve.wait_ge(s_x2_ps, g.count())
                            dve.wait_ge(s_x1_bias, g.count())
                            nc.vector.tensor_tensor(x2[:, :, :], tiles(bank_b), x1_bias[:, g.four], ALU.add).then_inc(s_x2, 1)
                            dve.wait_ge(s_x2, g.count())
                            stat(2, x2)
                            dve.wait_ge(s_stats[2], g.count(NT, NT))
                            settled(dve)
                            moment(2)
                            dve.wait_ge(s_mean[2], g.count())
                            nc.vector.tensor_scalar(var_eps[2][:, :], moments[2][:, :, 1], 1e-5, None, ALU.add)\
                                .then_inc(s_moments[2], 1)
                        if slot == SLOT["norm2"]:
                            dve.wait_ge(s_rstd[2], g.count())
                            normalise(2, x2)
                        if slot == SLOT["xt2_lo"]:
                            dve.wait_ge(s_xt_hi[2], g.count())
                            relu_lo(2, bank_g)
                        if slot == SLOT["x3"]:
                            dve.wait_ge(s_ah_ps, g.count())
                            dve.wait_ge(s_x2_bias, g.count())
                            scaled_add(x3, tiles(bank_g), near_inv[:, g.four], x2_bias, s_x3)
                            dve.wait_ge(s_x3, g.count())
                            stat(3, x3)
                            dve.wait_ge(s_stats[3], g.count(NT, NT))
                            settled(dve)
                            moment(3)
                            dve.wait_ge(s_mean[3], g.count())
                            nc.vector.tensor_scalar(var_eps[3][:, :], moments[3][:, :, 1], 1e-5, None, ALU.add)\
                                .then_inc(s_moments[3], 1)
                        if slot == SLOT["norm3"]:
                            dve.wait_ge(s_rstd[3], g.count())
                            normalise(3, x3)
                        if slot == SLOT["xt3_lo"]:
                            dve.wait_ge(s_xt_hi[3], g.count())
                            relu_lo(3, bank_g)
                        if slot == SLOT["e_bias"]:
                            dve.wait_ge(s_e_ps, g.count())
                            nc.vector.tensor_tensor(e_bias[:, :, :], bank_g[:, N:N + 2 * NT].rearrange("p (t n) -> p t n", t=NT),
                                                    e_const[:, :, :], ALU.add).then_inc(s_e_bias, 1)
                        if slot == SLOT["e_max"]:
                            dve.wait_ge(s_e, g.count())
                            nc.vector.tensor_tensor(e_max, e_pos, e_leak, ALU.max).then_inc(s_e_max, 1)
                        if slot == SLOT["a_inv"]:
                            dve.wait_ge(s_a_ps, g.count())
                            nc.vector.tensor_scalar(a_inv[:, 0, :], bank_b[:, 0:NT], 1e-12, None, ALU.add).then_inc(s_a_sum, 1)
                            dve.wait_ge(s_a_sum, g.count())
                            nc.vector.reciprocal(a_inv[:, 1, :], a_inv[:, 0, :]).then_inc(s_a_inv, 1)
                        if slot == SLOT["y1"]:
                            dve.wait_ge(s_y2_ps, g.count())
                            dve.wait_ge(s_xw1, g.count())
                            dve.wait_ge(s_a_inv, g.count())
                            scaled_add(y1, tiles(bank_g), a_inv[:, 1], xw1, s_y1)
                        if slot == SLOT["x_out"]:
                            dve.wait_ge(s_hop_ps, g.count())
                            dve.wait_ge(s_xw0_bias, g.count())
                            scaled_add(hid, tiles(bank_g), a_inv[:, 1], xw0_bias, s_hid)
                            dve.wait_ge(s_hid, g.count())
                            if not g.first:
                                dve.wait_ge(s_stored, g.before().count(16, 16))
                            nc.vector.scalar_tensor_tensor(out=flat(x_out[:, :, :]), in0=flat(hid[:, :, :]), scalar=0.0,
                                                           in1=flat(x3[:, :, :]), op0=ALU.max, op1=ALU.add).then_inc(s_out, 1)
                        if slot in (SLOT["c_rows_first"], SLOT["c_rows_last"]):
                            part = int(slot == SLOT["c_rows_last"])
                            dve.wait_ge(s_context, g.count(H, (part + 1) * HG))
                            at = slice(part * HG, (part + 1) * HG)
                            nc.vector.reciprocal(c_inv[:, :, at], ctx_ps[:, :, :, HD]).then_inc(s_c_inv, 1)
                            dve.wait_ge(s_c_inv, g.count(2, part + 1))
                            for r in range(NT):
                                last = nc.vector.tensor_tensor(
                                    c_rows[:, r, at, :], ctx_ps[:, r, :, 0:HD],
                                    c_inv[:, r, at].unsqueeze(2).broadcast_to([P, HG, HD]), ALU.mult)
                            last.then_inc(s_c_rows, 1)

            for t in range(AHEAD):
                iteration(0, t)
            with dve.Fori(0, ROUNDS) as i:
                for u in range(BODY):
                    iteration(i, AHEAD + u)
            for t in range(ALL - BEHIND, ALL):
                iteration(0, t)

        @block.tensor
        def _(pe):
            pe.wait_ge(s_setup, 1)

            def turn(dst, src):
                for k in range(2):
                    for r in range(2):
                        last = nc.tensor.transpose(dst[:, k * 256 + r * P:k * 256 + (r + 1) * P], src(r, k), ident[:, :])
                return last

            def split_product(dst, lhs, rhs):
                passes = [(k, p, q) for k in range(KT) for p, q in ((0, 0), (0, 1), (1, 0))]
                for n, (k, p, q) in enumerate(passes):
                    last = nc.tensor.matmul(dst, lhs(p, k), rhs(q, k), start=n == 0, stop=n == len(passes) - 1)
                return last

            def by_rows(dst, xt, name):
                w = w_hl[name]
                for r in range(NT):
                    last = split_product(dst[:, r], lambda p, k: xt[:, p, k, r * P:(r + 1) * P], lambda q, k: w[:, q, k, :])
                return last

            def by_cols(dst, xt, name):
                w = w_hl[name]
                for f in range(KT):
                    last = split_product(dst[:, f], lambda p, k: w[:, p, k, f * P:(f + 1) * P], lambda q, k: xt[:, q, k, :])
                return last

            def over_nodes(dst, lhs, rhs):
                for r in range(NT):
                    for k in range(NT):
                        last = nc.tensor.matmul(dst(r), lhs[:, k, r * P:(r + 1) * P], rhs(k), start=k == 0, stop=k == NT - 1)
                return last

            def norm_t(n, dst):
                turn(dst, lambda r, k: x_norm[n // 2][:, r, k * P:(k + 1) * P]).then_inc(s_xt_ps[n], 1)

            def scores(g, h):
                for r in range(NT):
                    last = nc.tensor.matmul(tiles(bank_s[h % 2])[:, r], q_stack[:, g.two, h, r * P:(r + 1) * P],
                                            k_stack[:, g.two, h, :], start=True, stop=True)
                last.then_inc(s_scores, 1)

            def context(g, h):
                for r in range(NT):
                    for k in range(NT):
                        last = nc.tensor.matmul(ctx_ps[:, r, h % HG, :], probs[:, h % 3, k * N + r * P:k * N + (r + 1) * P],
                                                v_heads[:, g.two, k, h, :], start=k == 0, stop=k == NT - 1)
                last.then_inc(s_context, 1)

            def iteration(i, t):
                xa, xc = xt_hl
                rows_a, rows_g, rows_b = tiles(bank_a), tiles(bank_g), tiles(bank_b)
                for s in range(SLOTS):
                    for slot, g in due(i, t, s):
                        if (h := head_at(slot, "scores_mm")) is not None:
                            if h == 0:
                                pe.wait_ge(s_stack, g.count(STACK, STACK))
                            if not g.first or h > 1:
                                pe.wait_ge(s_masked, g.count(H, h - 1))
                            scores(g, h)
                        if slot == SLOT["turn0"]:
                            if not g.first:
                                pe.wait_ge(s_v1, g.before().count())
                            pe.wait_ge(s_norm[0], g.count())
                            norm_t(0, bank_a)
                        if slot == SLOT["adj_turn"]:
                            pe.wait_ge(s_adj[g.four], g.round(4, 16))
                            pe.wait_ge(s_xt[0], g.count())
                            turn(bank_a, lambda r, k: adj_n[:, g.four, r, k * P:(k + 1) * P]).then_inc(s_adj_ps, 1)
                        if slot == SLOT["qk0_mm"]:
                            pe.wait_ge(s_adj_t, g.count())
                            by_rows(qk0_ps, xa, "qk0").then_inc(s_qk0_ps, 1)
                        if slot == SLOT["near_k_mm"]:
                            pe.wait_ge(s_qk0, g.count())
                            over_nodes(lambda r: ak_ps[:, r], adj_t[:, g.four],
                                       lambda k: qk0[:, k, Q0:2 * Q0 + 1]).then_inc(s_ak_ps, 1)
                        if slot == SLOT["w_all_mm"]:
                            pe.wait_ge(s_w_col, g.count())
                            for r in range(NT):
                                last = nc.tensor.matmul(bank_a[:, r * P:(r + 1) * P], w_col[:, r:r + 1].broadcast_to([P, P]),
                                                        ident[:, :], start=True, stop=True)
                            last.then_inc(s_w_ps, 1)
                        if slot == SLOT["v0_mm"]:
                            pe.wait_ge(s_w_exp, g.count())
                            by_rows(rows_a, xa, "v0").then_inc(s_v0_ps, 1)
                        if slot == SLOT["turn1"]:
                            pe.wait_ge(s_x1, g.count())
                            pe.wait_ge(s_norm[1], g.count())
                            norm_t(1, bank_a)
                        if slot == SLOT["q1_mm"]:
                            pe.wait_ge(s_xt[1], g.count())
                            by_cols(rows_a, xa, "q1").then_inc(s_q1_ps, 1)
                        if slot == SLOT["k1_mm"]:
                            pe.wait_ge(s_q1, g.count())
                            by_cols(rows_a, xa, "k1").then_inc(s_k1_ps, 1)
                        if slot == SLOT["v1_mm"]:
                            pe.wait_ge(s_k1, g.count())
                            by_rows(rows_a, xa, "v1").then_inc(s_v1_ps, 1)
                        if (h := head_at(slot, "scores_turn")) is not None:
                            pe.wait_ge(s_centred, g.count(H, h + 1))
                            if not g.first or h > 1:
                                pe.wait_ge(s_probs, g.count(H, h - 1))
                            turn(bank_t[h % 2], lambda r, k: centred[:, h % 3, r * N + k * P:r * N + (k + 1) * P])\
                                .then_inc(s_scores_t, 1)
                        if slot == SLOT["c_turn"]:
                            pe.wait_ge(s_c_rows, g.count(2, 2))
                            if not g.first:
                                pe.wait_ge(s_a_inv, g.before().count())
                            turn(bank_b, lambda r, k: c_rows[:, r, k * HG:(k + 1) * HG, :].rearrange("p h e -> p (h e)"))\
                                .then_inc(s_cols_ps, 1)
                        if slot == SLOT["x2_mm"]:
                            pe.wait_ge(s_c_cols, g.count())
                            for r in range(NT):
                                for k in range(KT):
                                    last = nc.tensor.matmul(rows_b[:, r], c_cols[:, k, r * P:(r + 1) * P], wo_sb[:, k, :],
                                                            start=k == 0, stop=k == KT - 1)
                            last.then_inc(s_x2_ps, 1)
                        if slot == SLOT["turn2"]:
                            if not g.first:
                                pe.wait_ge(s_hid, g.before().count())
                            pe.wait_ge(s_norm[2], g.count())
                            norm_t(2, bank_g)
                        if slot == SLOT["h2_mm"]:
                            pe.wait_ge(s_xt[2], g.count())
                            by_rows(rows_g, xc, "n2").then_inc(s_h2_ps, 1)
                        if slot == SLOT["x3_mm"]:
                            pe.wait_ge(s_h2, g.count())
                            over_nodes(lambda r: rows_g[:, r], adj_t[:, g.four], lambda k: h2[:, k, :]).then_inc(s_ah_ps, 1)
                        if slot == SLOT["turn3"]:
                            pe.wait_ge(s_x3, g.count())
                            pe.wait_ge(s_norm[3], g.count())
                            norm_t(3, bank_g)
                        if slot == SLOT["edge_mm"]:
                            pe.wait_ge(s_xt[3], g.count())
                            split_product(bank_g[:, 0:N], lambda p, k: si_hl[:, p, k, :], lambda q, k: xc[:, q, k, :])
                            for r in range(NT):
                                last = split_product(bank_g[:, N + 2 * r:N + 2 * r + 2],
                                                     lambda p, k: xc[:, p, k, r * P:(r + 1) * P],
                                                     lambda q, k: sj_hl[:, q, k, :])
                            last.then_inc(s_e_ps, 1)
                        if slot == SLOT["xw2_mm"]:
                            pe.wait_ge(s_e, g.count())
                            by_rows(rows_g, xc, "h2").then_inc(s_xw2_ps, 1)
                        if slot == SLOT["xw1_mm"]:
                            pe.wait_ge(s_xw2, g.count())
                            by_rows(rows_g, xc, "h1").then_inc(s_xw1_ps, 1)
                        if slot == SLOT["a_sum_mm"]:
                            pe.wait_ge(s_alpha, g.count())
                            pe.wait_ge(s_x2, g.count())
                            over_nodes(lambda r: bank_b[:, r:r + 1], alpha, lambda k: ones[:, 0:1]).then_inc(s_a_ps, 1)
                        if slot == SLOT["y1_mm"]:
                            pe.wait_ge(s_xw1, g.count())
                            pe.wait_ge(s_alpha, g.count())
                            over_nodes(lambda r: rows_g[:, r], alpha, lambda k: xw2[:, k, :]).then_inc(s_y2_ps, 1)
                        if slot == SLOT["xw0_mm"]:
                            pe.wait_ge(s_y1, g.count())
                            by_rows(rows_g, xc, "h0").then_inc(s_xw0_ps, 1)
                        if slot == SLOT["hid_mm"]:
                            pe.wait_ge(s_xw0, g.count())
                            over_nodes(lambda r: rows_g[:, r], alpha, lambda k: y1[:, k, :]).then_inc(s_hop_ps, 1)
                        if (h := head_at(slot, "context_mm")) is not None:
                            pe.wait_ge(s_probs, g.count(H, h + 1))
                            if h == 0:
                                pe.wait_ge(s_v1, g.count())
                            if h == HG or h == 0 and not g.first:
                                pe.wait_ge(s_c_rows, g.count(2, h // HG))
                            context(g, h)

            for t in range(AHEAD):
                iteration(0, t)
            with pe.Fori(0, ROUNDS) as i:
                for u in range(BODY):
                    iteration(i, AHEAD + u)
            for t in range(ALL - BEHIND, ALL):
                iteration(0, t)


_OUT = (32, 256, 256)


def kernel(**inputs):
    import numpy as _np
    import concourse.bacc as _bacc
    from concourse import mybir as _mybir
    from concourse.bass_utils import run_bass_kernel_spmd as _run

    turned = {"L0_gnn_W_qk", "L0_gnn_W_v", "L1_gnn_Wq", "L1_gnn_Wk", "L1_gnn_Wv", "L1_gnn_Wo"}
    order = ["x", "adj", "L0_gnn_W_qk", "L0_gnn_W_v", "L1_gnn_Wq", "L1_gnn_bq", "L1_gnn_Wk", "L1_gnn_bk",
             "L1_gnn_Wv", "L1_gnn_bv", "L1_gnn_Wo", "L1_gnn_bo", "L2_gnn_W", "L2_gnn_b", "L3_gnn_Wv",
             "L3_gnn_bv", "L3_gnn_aw", "L3_gnn_ab", "L3_gnn_Wk", "L3_gnn_bk"]
    nc = _bacc.Bacc("TRN2", target_bir_lowering=False, num_devices=1)
    arrays, args = {}, []
    for name in order:
        a = _np.asarray(inputs[name])
        a = _np.ascontiguousarray(a.T if name in turned else a)
        arrays[f"in_{name}"] = a
        args.append(nc.dram_tensor(f"in_{name}", a.shape, _mybir.dt.from_np(a.dtype), kind="ExternalInput").ap())
    args.append(nc.dram_tensor("out_x", _OUT, _mybir.dt.float32, kind="ExternalOutput").ap())
    graph_layers_kernel(nc, *args)
    r = _run(nc, [arrays], core_ids=[0])
    return r.results[0]["out_x"]
```

```python
from contextlib import ExitStack

import concourse.bass as bass
from concourse import mybir

F32 = mybir.dt.float32
F32R = mybir.dt.float32r
ALU = mybir.AluOpType
ACT = mybir.ActivationFunctionType
AX_X = mybir.AxisListType.X

P = 128
BODY = 4
SLOTS = 128
DEPTH = 5
LEAST = -3.0e38

SLOT = {
    "load": 0, "moments0": 36, "rstd0": 56, "norm0": 67, "adj_turn": 62, "adj_t": 67, "turn0": 69,
    "xt0_hi": 76, "xt0_lo": 77, "v0_mm": 82, "vqk0": 91, "near_k_mm": 106, "w_own": 115,
    "w_all_mm": 119, "w_max": 122, "w_exp": 127, "w_prob": 130, "x1": 138, "x1_bias": 171,
    "rstd1": 143, "norm1": 145, "turn1": 150, "xt1_hi": 151, "xt1_lo": 154, "q1_mm": 162,
    "q1_hi": 165, "q1_lo": 167, "k1_mm": 163, "k1_hi": 165, "k1_lo": 174, "v1_mm": 173, "v1": 180,
    "qk_stack": 204, "scores_mm": 215, "masked": 224, "centred": 230, "scores_turn": 236,
    "probs": 243, "context_mm": 256, "c_rows_first": 311, "c_rows_last": 382, "c_turn": 387,
    "c_hi": 389, "c_lo": 396, "x2_mm": 402, "x2": 415, "x2_bias": 462, "rstd2": 422, "norm2": 434,
    "turn2": 439, "xt2_hi": 440, "xt2_lo": 445, "h2_mm": 447, "h2_hi": 456, "h2_lo": 460,
    "adj_hi": 403, "adj_lo": 455, "x3_mm": 462, "x3": 473, "rstd3": 485, "norm3": 488, "turn3": 491,
    "xt3_hi": 495, "xt3_lo": 503, "xw2_mm": 507, "xw2_hi": 513, "xw2_lo": 517, "edge_mm": 525,
    "edge_exp": 529, "e_max": 531, "alpha": 544, "alpha_hi": 546, "alpha_lo": 547, "xw1_mm": 529,
    "xw1": 547, "y1_mm": 549, "y1": 551, "y1_hi": 553, "y1_lo": 555, "xw0_mm": 558, "xw0": 561,
    "xw0_bias": 580, "hid_mm": 568, "x_out": 581, "store": 608,
}
SPLIT_AT = (81, 101, 121, 141, 181, 184, 187, 190, 193)
EDGE_WEIGHTS_AT = 221
HEAD_STEP = SLOTS // 8


class Graph:

    def __init__(self, i, c):
        self.i, self.c = i, c
        self.two, self.four = c % 2, c % 4
        self.first = isinstance(i, int) and c == 0

    def number(self):
        return BODY * self.i + self.c

    def count(self, each=1, events=1):
        return BODY * each * self.i + (each * self.c + events)

    def round(self, ring, each):
        return each * (BODY // ring) * self.i + each * (self.c // ring + 1)

    def before(self, n=1):
        return Graph(self.i, self.c - n)


def graph_layers_kernel(nc, x, adj, w_qk0, w_v0, w_q1, b_q1, w_k1, b_k1, w_v1, b_v1, w_o1, b_o1,
                        w2, b2, w_v3, b_v3, a_w3, a_b3, w_k3, b_k3, out):
    G, N, D = x.shape
    NT, KT = N // P, D // P
    Q0 = w_qk0.shape[1] // 2
    H = 8
    HD = D // H
    HE = HD + 1
    HG = P // HD
    HEADS = [t * HG + j for j in range(HG) for t in range(KT)]
    HOPS = w_k3.shape[0]
    SCALE0 = float(Q0) ** -0.5
    SCALE1 = 2.0 * float(HD) ** -0.5
    ALL = G + DEPTH - 1
    AHEAD, BEHIND = -(-DEPTH // BODY) * BODY, DEPTH - 1
    ROUNDS = (ALL - AHEAD - BEHIND) // BODY
    assert (ALL - AHEAD - BEHIND) % BODY == 0 and NT == 2 and KT == 2

    with ExitStack() as ctx:
        def sb(name, shape, dt=F32):
            return ctx.enter_context(nc.sbuf_tensor(name, shape, dt))

        def bank(name):
            return ctx.enter_context(nc.psum_tensor(name, [P, 512], F32))

        def sem(name):
            return ctx.enter_context(nc.semaphore(name))

        x0 = sb("x0", [P, 2, NT, D])
        adj_n = sb("adj_n", [P, 4, NT, N])
        adj_t = sb("adj_t", [P, 4, NT, N])
        x1_bias = sb("x1_bias", [P, 4, NT, D])
        near_inv = sb("near_inv", [P, 4, NT])
        q_stack = sb("q_stack", [P, 2, H, N], F32R)
        k_stack = sb("k_stack", [P, 2, H, N], F32R)
        v_heads = sb("v_heads", [P, 2, NT, H, HE])
        x_out = sb("x_out", [P, NT, D])

        x1 = sb("x1", [P, NT, D])
        vqk0 = sb("vqk0", [P, NT, D + 2 * Q0 + 1])
        qak = sb("qak", [P, NT, Q0])
        w_col = sb("w_col", [P, NT])
        w_neg = sb("w_neg", [P, 2])
        w_exp = sb("w_exp", [P, N])
        w_sum = sb("w_sum", [P, 2])
        w_e = sb("w_e", [P, NT])
        w_prob = sb("w_prob", [P, NT])
        q_hl = sb("q_hl", [P, 2, KT, N], F32R)
        k_hl = sb("k_hl", [P, 2, KT, N], F32R)

        heads = sb("heads", [P, 9, NT * N])
        masked, centred, probs = heads[:, 0:3, :], heads[:, 3:6, :], heads[:, 6:9, :]
        s_top = sb("s_top", [P, 3, NT])
        c_inv = sb("c_inv", [P, NT, H])
        c_rows = sb("c_rows", [P, NT, H, HD])
        c_hl = sb("c_hl", [P, 2, KT, N], F32R)
        x2 = sb("x2", [P, NT, D])
        x2_bias = sb("x2_bias", [P, NT, D])

        adj_hl = sb("adj_hl", [P, 2, NT, N], F32R)
        h2_hl = sb("h2_hl", [P, 2, NT, D], F32R)
        x3 = sb("x3", [P, NT, D])
        e_bias = sb("e_bias", [P, NT, 3])
        edges = sb("edges", [P, 4, NT, N])
        e_pos, e_leak, e_max, alpha = (edges[:, n] for n in range(4))
        a_inv = sb("a_inv", [P, 2, NT])
        xw2_hl = sb("xw2_hl", [P, 2, NT, D + 2], F32R)
        alpha_hl = sb("alpha_hl", [P, 2, NT, N], F32R)
        y1_hl = sb("y1_hl", [P, 2, NT, D], F32R)
        xw1 = sb("xw1", [P, NT, D])
        xw0 = sb("xw0", [P, NT, D])
        xw0_bias = sb("xw0_bias", [P, NT, D])
        y1 = sb("y1", [P, NT, D])
        hid = sb("hid", [P, NT, D])

        x_norm = [sb(f"x_norm{n}", [P, NT, D]) for n in range(2)]
        xt_hl = [sb(f"xt_hl{n}", [P, 2, KT, N], F32R) for n in range(2)]
        stats = [sb(f"stats{n}", [P, NT, 6]) for n in range(4)]
        moments = [sb(f"moments{n}", [P, NT, 2]) for n in range(4)]
        var_eps = [sb(f"var_eps{n}", [P, NT]) for n in range(4)]
        rstd = [sb(f"rstd{n}", [P, NT]) for n in range(4)]

        beside = {"v0": 2 * Q0, "h2": 4}
        w_src = {"v0": w_v0, "q1": w_q1, "k1": w_k1, "v1": w_v1, "o1": w_o1, "n2": w2,
                 "h2": w_k3[2], "h1": w_k3[1], "h0": w_k3[0]}
        w_hl = {k: sb("w_" + k, [P, 2, KT, D + beside.get(k, 0)], F32R) for k in w_src}
        w_qk = sb("w_qk", [P, KT, 2 * Q0])
        bo_row = sb("bo_row", [P, D])
        bv_row = sb("bv_row", [P, D])
        b2_row = sb("b2_row", [P, D])
        bk_row = sb("bk_row", [P, D])
        bqk_col = sb("bqk_col", [P, 2, KT])
        e_const = sb("e_const", [P, NT, 3])
        a_part = sb("a_part", [P, 8])
        ident = sb("ident", [P, P])
        ones = sb("ones", [P, P])
        half = sb("half", [P, NT])

        bank_s = bank("bank_s")
        bank_t = bank("bank_t")
        bank_c = bank("bank_c")
        bank_a = [bank("bank_a0"), bank("bank_a1")]
        bank_b = bank("bank_b")
        bank_g = [bank("bank_g0"), bank("bank_g1")]
        ctx_ps = bank_c[:, 0:NT * HG * HE].rearrange("p (t h e) -> p t h e", t=NT, h=HG)

        def tiles(b):
            return b[:, :].rearrange("p (t n) -> p t n", t=2)

        s_weights = [sem(f"s_weight{n}") for n in range(len(w_src))]
        s_biases, s_rows = sem("s_biases"), sem("s_rows")
        s_made = sem("s_made")
        s_ident = sem("s_ident")
        s_ones = sem("s_ones")
        s_weight_hi = sem("s_weight_hi")
        s_split = sem("s_split")
        s_carry = sem("s_carry")
        s_x = [sem(f"s_x_in{n}") for n in range(2)]
        s_adj = [sem(f"s_adj_in{n}") for n in range(4)]
        s_stats = [sem(f"s_stats{n}") for n in range(4)]
        s_moments = [sem(f"s_moments{n}") for n in range(4)]
        s_mean = [sem(f"s_mean{n}") for n in range(4)]
        s_rstd = [sem(f"s_rstd{n}") for n in range(4)]
        s_norm = [sem(f"s_norm{n}") for n in range(4)]
        s_xt_ps = [sem(f"s_xt_ps{n}") for n in range(4)]
        s_xt_hi = [sem(f"s_xt_hi{n}") for n in range(4)]
        s_xt = [sem(f"s_xt{n}") for n in range(4)]
        s_adj_ps, s_adj_t = sem("s_adj_ps"), sem("s_adj_t")
        s_v0_ps, s_vqk0 = sem("s_v0_ps"), sem("s_vqk0")
        s_ak_ps, s_w_col = sem("s_ak_ps"), sem("s_w_col")
        s_w_max = sem("s_w_max")
        s_w_ps, s_w_neg, s_w_exp, s_w_inv, s_w_prob = (
            sem("s_w_ps"), sem("s_w_neg"), sem("s_w_exp"), sem("s_w_inv"), sem("s_w_prob"))
        s_x1, s_x1_bias = sem("s_x1"), sem("s_x1_bias")
        s_q1_ps, s_q1_hi, s_q1 = sem("s_q1_ps"), sem("s_q1_hi"), sem("s_q1")
        s_k1_ps, s_k1_hi, s_k1 = sem("s_k1_ps"), sem("s_k1_hi"), sem("s_k1")
        s_v1_ps, s_v1 = sem("s_v1_ps"), sem("s_v1")
        s_stack = [sem(f"s_stack{j}") for j in range(HG)]
        s_scores, s_masked, s_centred, s_scores_t, s_probs, s_context = (
            sem("s_scores"), sem("s_masked"), sem("s_centred"), sem("s_scores_t"), sem("s_probs"),
            sem("s_context"))
        s_c_inv, s_c_rows, s_cols_ps, s_c_hi, s_c, s_x2_ps, s_x2, s_x2_bias = (
            sem("s_c_inv"), sem("s_c_rows"), sem("s_cols_ps"), sem("s_c_hi"), sem("s_c"), sem("s_x2_ps"),
            sem("s_x2"), sem("s_x2_bias"))
        s_adj_hi, s_adj_hl = sem("s_adj_hi"), sem("s_adj_hl")
        s_h2_ps, s_h2_hi, s_h2, s_ah_ps, s_x3 = (
            sem("s_h2_ps"), sem("s_h2_hi"), sem("s_h2"), sem("s_ah_ps"), sem("s_x3"))
        s_e_ps, s_e_bias, s_e, s_e_max, s_alpha = (
            sem("s_e_ps"), sem("s_e_bias"), sem("s_e"), sem("s_e_max"), sem("s_alpha"))
        s_a_sum, s_a_inv = sem("s_a_sum"), sem("s_a_inv")
        s_xw2_ps, s_xw2_hi, s_xw1_ps, s_xw1, s_xw0_ps, s_xw0, s_xw0_bias = (
            sem("s_xw2_ps"), sem("s_xw2_hi"), sem("s_xw1_ps"), sem("s_xw1"), sem("s_xw0_ps"),
            sem("s_xw0"), sem("s_xw0_bias"))
        s_alpha_hi, s_alpha_hl, s_y1_hi, s_y1_hl = (
            sem("s_alpha_hi"), sem("s_alpha_hl"), sem("s_y1_hi"), sem("s_y1_hl"))
        s_y2_ps, s_y1, s_hop_ps, s_hid, s_out = (
            sem("s_y2_ps"), sem("s_y1"), sem("s_hop_ps"), sem("s_hid"), sem("s_out"))
        s_stored = sem("s_stored")

        block = ctx.enter_context(nc.Block())

        def due(i, t, s):
            inside = not isinstance(i, int)
            return [(n * SLOTS + s, Graph(i, t - n)) for n in range(DEPTH) if inside or 0 <= t - n < G]

        def head_at(slot, step):
            h, off = divmod(slot - SLOT[step], HEAD_STEP)
            return h if off == 0 and 0 <= h < H else None

        def settled(eng):
            eng.sem_inc(s_carry, 1)

        def flat(ap):
            return ap.rearrange("p t n -> p (t n)")

        ak_ps = bank_a[0][:, 0:NT * (Q0 + 1)].rearrange("p (t n) -> p t n", t=NT)
        hid_rows = [flat(hid[:, :, :])[:, 0:D], flat(hid[:, :, :])[:, D:2 * D], flat(y1[:, :, :])[:, 0:D]]
        STACK = 2 * HG * 16

        @block.sync
        def _(sp):
            def load(g):
                if g.c >= 2:
                    sp.wait_ge(s_x1, g.before(2).count())
                    settled(sp)
                    if g.c >= 4:
                        sp.wait_ge(s_masked, g.before(4).count(H, H))
                        settled(sp)
                at = bass.ds(g.number(), 1)
                sp.dma_start(x0[:, g.two, :, :], x[at].rearrange("a (t p) d -> p (a t) d", p=P))\
                    .then_inc(s_x[g.two], 16)
                sp.dma_start(adj_n[:, g.four, :, :], adj[at].rearrange("a (t p) d -> p (a t) d", p=P))\
                    .then_inc(s_adj[g.four], 16)

            load(Graph(0, 0))
            sp.dma_start(w_qk[:, :, :], w_qk0.rearrange("(k p) n -> p k n", p=P)).then_inc(s_weights[0], 16)
            for n, src in enumerate(w_src.values()):
                dst = heads[:, n, :].rearrange("p (k n) -> p k n", k=KT)
                sp.dma_start(dst, src.rearrange("(k p) n -> p k n", p=P)).then_inc(s_weights[n], 16)
            for n, src in enumerate((b_q1, b_k1)):
                sp.dma_start(bqk_col[:, n, :], src.rearrange("(k p) -> p k", p=P),
                             allow_slow_non_contiguous=True).then_inc(s_biases, 16)
            for row, src in ((bo_row, b_o1), (bv_row, b_v1), (b2_row, b2)):
                sp.dma_start(row[:, :], src.rearrange("(o n) -> o n", o=1).broadcast_to([P, D])).then_inc(s_biases, 16)
            sp.dma_start(e_pos, w_v3.rearrange("(k p) n -> p k n", p=P)).then_inc(s_rows, 16)
            sp.dma_start(e_leak, a_w3.rearrange("(o t n) u -> o t (n u)", o=1, t=2).broadcast_to([P, 2, D])).then_inc(s_rows, 16)
            sp.dma_start(e_max[:, 0], b_v3.rearrange("(o n) -> o n", o=1).broadcast_to([P, D])).then_inc(s_rows, 16)
            sp.dma_start(a_part[:, 7:8], a_b3.rearrange("(o n) -> o n", o=1).broadcast_to([P, 1])).then_inc(s_rows, 16)
            for n in range(HOPS):
                sp.dma_start(hid_rows[n], b_k3[n:n + 1, :].broadcast_to([P, D])).then_inc(s_rows, 16)

            def stack(g):
                for j in range(HG):
                    for src, dst, order in ((q_hl, q_stack, (0, 1, 0, 1)), (k_hl, k_stack, (0, 0, 1, 1))):
                        for c in range(HG):
                            sp.dma_start(
                                dst[c * HD:(c + 1) * HD, g.two, j::HG, :].bitcast(F32),
                                src[j * HD:(j + 1) * HD, order[c], :, :].bitcast(F32)).then_inc(s_stack[j], 16)

            def store(g):
                sp.wait_ge(s_out, g.count())
                settled(sp)
                at = bass.ds(g.number(), 1)
                sp.dma_start(out[at].rearrange("a (t p) d -> p (a t) d", p=P), x_out[:, :, :]).then_inc(s_stored, 16)

            def iteration(i, t):
                for s in range(SLOTS):
                    for slot, g in due(i, t, s):
                        if slot == SLOT["load"] and not g.first:
                            load(g)
                        if slot == SLOT["qk_stack"]:
                            sp.wait_ge(s_q1, g.count())
                            settled(sp)
                            sp.wait_ge(s_k1, g.count())
                            settled(sp)
                            stack(g)
                        if slot == SLOT["store"]:
                            store(g)

            for t in range(AHEAD):
                iteration(0, t)
            with sp.Fori(0, ROUNDS) as i:
                for u in range(BODY):
                    iteration(i, AHEAD + u)
            for t in range(ALL - BEHIND, ALL):
                iteration(0, t)
            sp.wait_ge(s_stored, 16 * G)

        @block.gpsimd
        def _(pool):
            nc.gpsimd.memset(ident[:, :], 0.0).then_inc(s_ident, 1)
            nc.gpsimd.memset(half[:, :], -0.5).then_inc(s_ident, 1)
            pool.wait_ge(s_ident, 2)
            nc.gpsimd.affine_select(out=ident[:, :], in_=ident[:, :], compare_op=ALU.not_equal, fill=1.0,
                                    base=0, pattern=[[-1, P]], channel_multiplier=1).then_inc(s_ident, 1)

            def add_row(dst, src, row, done):
                for r in range(NT):
                    last = nc.gpsimd.tensor_tensor(dst[:, r, :], src[:, r, :], row[:, :], ALU.add)
                last.then_inc(done, 1)

            def centre(h):
                for r in range(NT):
                    at = slice(r * N, (r + 1) * N)
                    last = nc.gpsimd.tensor_scalar(centred[:, h % 3, at], masked[:, h % 3, at], -1.0,
                                                   s_top[:, h % 3, r:r + 1], ALU.mult, ALU.add)
                last.then_inc(s_centred, 1)

            def iteration(i, t):
                for s in range(SLOTS):
                    for slot, g in due(i, t, s):
                        if (h := head_at(slot, "centred")) is not None:
                            pool.wait_ge(s_masked, g.count(H, h + 1))
                            settled(pool)
                            centre(h)
                        for n in range(4):
                            if slot == SLOT[f"rstd{n}"]:
                                pool.wait_ge(s_moments[n], g.count())
                                nc.gpsimd.tensor_tensor(rstd[n][:, :], var_eps[n][:, :], half[:, :], ALU.pow)\
                                    .then_inc(s_rstd[n], 1)
                        if slot == SLOT["x1_bias"]:
                            pool.wait_ge(s_x1, g.count())
                            if g.first:
                                pool.wait_ge(s_biases, 16 * 5)
                            add_row(x1_bias[:, g.four], x1, bo_row, s_x1_bias)
                        if slot == SLOT["x2_bias"]:
                            pool.wait_ge(s_x2, g.count())
                            add_row(x2_bias, x2, b2_row, s_x2_bias)
                        if slot == SLOT["alpha"]:
                            pool.wait_ge(s_e_max, g.count())
                            nc.gpsimd.tensor_tensor(alpha, e_max, adj_t[:, g.four], ALU.mult).then_inc(s_alpha, 1)
                        if slot == SLOT["adj_lo"]:
                            pool.wait_ge(s_adj_hi, g.count())
                            nc.gpsimd.tensor_tensor(adj_hl[:, 1], adj_t[:, g.four], adj_hl[:, 0].bitcast(F32), ALU.subtract)\
                                .then_inc(s_adj_hl, 1)
                        if slot == SLOT["alpha_lo"]:
                            pool.wait_ge(s_alpha_hi, g.count())
                            nc.gpsimd.tensor_tensor(alpha_hl[:, 1], alpha, alpha_hl[:, 0].bitcast(F32), ALU.subtract)\
                                .then_inc(s_alpha_hl, 1)
                        if slot == SLOT["y1_lo"]:
                            pool.wait_ge(s_y1_hi, g.count())
                            nc.gpsimd.tensor_tensor(y1_hl[:, 1], y1[:, :, :], y1_hl[:, 0].bitcast(F32), ALU.subtract)\
                                .then_inc(s_y1_hl, 1)
                        if slot == SLOT["xw0_bias"]:
                            pool.wait_ge(s_xw0, g.count())
                            add_row(xw0_bias, xw0, bk_row, s_xw0_bias)

            for t in range(AHEAD):
                iteration(0, t)
            with pool.Fori(0, ROUNDS) as i:
                for u in range(BODY):
                    iteration(i, AHEAD + u)
            for t in range(ALL - BEHIND, ALL):
                iteration(0, t)

        @block.scalar
        def _(act):
            def weight_hi(n, name):
                act.wait_ge(s_weights[n], 32 if name == "v0" else 16)
                if name == "v0":
                    nc.scalar.activation(w_hl[name][:, 0, :, D:], w_qk[:, :, :], ACT.Copy)
                nc.scalar.activation(w_hl[name][:, 0, :, 0:D], heads[:, n, :].rearrange("p (k n) -> p k n", k=KT),
                                     ACT.Copy).then_inc(s_weight_hi, 1)

            def relu_hi(n, src):
                nc.scalar.activation(flat(xt_hl[n // 2][:, 0]), src[:, :], ACT.Relu).then_inc(s_xt_hi[n], 1)

            def bias_hi(dst, col, done):
                for k in range(KT):
                    last = nc.scalar.activation(dst[:, 0, k, :], tiles(bank_a[col])[:, k], ACT.Identity,
                                                bias=bqk_col[:, col, k:k + 1])
                last.then_inc(done, 1)

            def iteration(i, t):
                for s in range(SLOTS):
                    if isinstance(i, int) and t * SLOTS + s in SPLIT_AT:
                        n = SPLIT_AT.index(t * SLOTS + s)
                        weight_hi(n, list(w_src)[n])
                    for slot, g in due(i, t, s):
                        if slot == SLOT["xt0_hi"]:
                            act.wait_ge(s_xt_ps[0], g.count())
                            relu_hi(0, bank_a[0])
                        if slot == SLOT["adj_t"]:
                            act.wait_ge(s_adj_ps, g.count())
                            nc.scalar.activation(adj_t[:, g.four], tiles(bank_a[1]), ACT.Copy).then_inc(s_adj_t, 1)
                        if slot == SLOT["vqk0"]:
                            act.wait_ge(s_v0_ps, g.count())
                            for r in range(NT):
                                last = nc.scalar.activation(vqk0[:, r, 0:D + 2 * Q0], bank_a[r][:, 0:D + 2 * Q0], ACT.Copy)
                            last.then_inc(s_vqk0, 1)
                        if slot == SLOT["w_exp"]:
                            act.wait_ge(s_w_neg, g.count())
                            nc.scalar.activation(w_exp[:, :], bank_a[1][:, 0:N], ACT.Exp, bias=w_neg[:, 1:2], scale=SCALE0,
                                                 accum_out=w_sum[:, 0:1])
                            nc.scalar.activation(w_e[:, :], w_col[:, :], ACT.Exp, bias=w_neg[:, 1:2], scale=SCALE0)\
                                .then_inc(s_w_exp, 1)
                        if slot == SLOT["xt1_hi"]:
                            act.wait_ge(s_xt_ps[1], g.count())
                            relu_hi(1, bank_a[0])
                        if slot == SLOT["q1_hi"]:
                            act.wait_ge(s_q1_ps, g.count())
                            if g.first:
                                act.wait_ge(s_biases, 16 * 5)
                            else:
                                for j in range(HG):
                                    act.wait_ge(s_stack[j], g.before().count(STACK, STACK))
                            bias_hi(q_hl, 0, s_q1_hi)
                        if slot == SLOT["k1_hi"]:
                            act.wait_ge(s_k1_ps, g.count())
                            bias_hi(k_hl, 1, s_k1_hi)
                        if (h := head_at(slot, "probs")) is not None:
                            act.wait_ge(s_scores_t, g.count(H, h + 1))
                            nc.scalar.activation(probs[:, h % 3], bank_t[:, :], ACT.Exp, scale=-1.0)\
                                .then_inc(s_probs, 1)
                        if slot == SLOT["c_hi"]:
                            act.wait_ge(s_cols_ps, g.count())
                            nc.scalar.activation(c_hl[:, 0], tiles(bank_b), ACT.Copy).then_inc(s_c_hi, 1)
                        if slot == SLOT["xt2_hi"]:
                            act.wait_ge(s_xt_ps[2], g.count())
                            relu_hi(2, bank_g[0])
                        if slot == SLOT["adj_hi"]:
                            act.wait_ge(s_adj_t, g.count())
                            nc.scalar.activation(adj_hl[:, 0], adj_t[:, g.four], ACT.Copy).then_inc(s_adj_hi, 1)
                        if slot == SLOT["h2_hi"]:
                            act.wait_ge(s_h2_ps, g.count())
                            nc.scalar.activation(h2_hl[:, 0], tiles(bank_g[0]), ACT.Copy).then_inc(s_h2_hi, 1)
                        if slot == SLOT["xt3_hi"]:
                            act.wait_ge(s_xt_ps[3], g.count())
                            relu_hi(3, bank_g[0])
                        if slot == SLOT["edge_exp"]:
                            act.wait_ge(s_e_bias, g.count())
                            act.wait_ge(s_e_ps, g.count())
                            for r in range(NT):
                                nc.scalar.activation(e_pos[:, r, :], bank_g[0][:, 0:N], ACT.Exp, bias=e_bias[:, r, 0:1])
                                last = nc.scalar.activation(e_leak[:, r, :], bank_g[0][:, 0:N], ACT.Exp,
                                                            bias=e_bias[:, r, 1:2], scale=0.2)
                            last.then_inc(s_e, 1)
                        if slot == SLOT["xw2_hi"]:
                            act.wait_ge(s_xw2_ps, g.count())
                            for r in range(NT):
                                last = nc.scalar.activation(xw2_hl[:, 0, r, 0:D], bank_g[r][:, 0:D], ACT.Copy)
                            last.then_inc(s_xw2_hi, 1)
                        if slot == SLOT["alpha_hi"]:
                            act.wait_ge(s_alpha, g.count())
                            nc.scalar.activation(alpha_hl[:, 0], alpha, ACT.Copy).then_inc(s_alpha_hi, 1)
                        if slot == SLOT["y1_hi"]:
                            act.wait_ge(s_y1, g.count())
                            nc.scalar.activation(y1_hl[:, 0], y1[:, :, :], ACT.Copy).then_inc(s_y1_hi, 1)
                        if slot == SLOT["xw1"]:
                            act.wait_ge(s_xw1_ps, g.count())
                            nc.scalar.activation(xw1[:, :, :], tiles(bank_g[1]), ACT.Copy).then_inc(s_xw1, 1)
                        if slot == SLOT["xw0"]:
                            act.wait_ge(s_xw0_ps, g.count())
                            nc.scalar.activation(xw0[:, :, :], tiles(bank_g[0]), ACT.Copy).then_inc(s_xw0, 1)

            for t in range(AHEAD):
                iteration(0, t)
            with act.Fori(0, ROUNDS) as i:
                for u in range(BODY):
                    iteration(i, AHEAD + u)
            for t in range(ALL - BEHIND, ALL):
                iteration(0, t)

        @block.vector
        def _(dve):
            made = [0]

            def then(ins):
                made[0] += 1
                ins.then_inc(s_made, 1)
                dve.wait_ge(s_made, made[0])

            def weight_lo(n, name):
                dve.wait_ge(s_weight_hi, n + 1)
                hl = w_hl[name]
                if name == "v0":
                    nc.vector.tensor_tensor(hl[:, 1, :, D:], w_qk[:, :, :], hl[:, 0, :, D:].bitcast(F32), ALU.subtract)
                nc.vector.tensor_tensor(hl[:, 1, :, 0:D], heads[:, n, :].rearrange("p (k n) -> p k n", k=KT),
                                        hl[:, 0, :, 0:D].bitcast(F32), ALU.subtract).then_inc(s_split, 1)

            def edge_weights():
                dve.wait_ge(s_rows, 16 * (4 + HOPS))
                spare = [buf[:, r, :] for buf in (x2, x3, xw1) for r in range(NT)]
                for k in range(KT):
                    for n in range(2):
                        nc.vector.tensor_tensor_reduce(spare[2 * k + n], e_pos[:, k, :], e_leak[:, n, :], 1.0, 0.0,
                                                       ALU.mult, ALU.add, a_part[:, 2 * k + n:2 * k + n + 1])
                nc.vector.tensor_tensor_reduce(spare[4], e_max[:, 0, :], e_leak[:, 0, :], 1.0, 0.0,
                                               ALU.mult, ALU.add, a_part[:, 4:5])
                nc.vector.tensor_tensor(bk_row[:, :], hid_rows[0], hid_rows[1], ALU.add)
                then(nc.vector.tensor_tensor_reduce(spare[5], e_max[:, 0, :], e_leak[:, 1, :], 1.0, 0.0,
                                                    ALU.mult, ALU.add, a_part[:, 5:6]))
                for k in range(KT):
                    for n in range(2):
                        for m, share in enumerate((1.0, 0.2)):
                            last = nc.vector.tensor_scalar(spare[k][:, 2 * n + m:2 * n + m + 1],
                                                           a_part[:, 2 * k + n:2 * k + n + 1], share, None, ALU.mult)
                then(last)
                edge = [w_hl["h2"][:, :, k, D:] for k in range(KT)]
                for k in range(KT):
                    last = nc.vector.tensor_copy(edge[k][:, 0], spare[k][:, 0:4])
                then(last)
                for k in range(KT):
                    nc.vector.tensor_tensor(edge[k][:, 1], spare[k][:, 0:4], edge[k][:, 0].bitcast(F32), ALU.subtract)
                then(nc.vector.tensor_tensor(a_part[:, 6:7], a_part[:, 4:5], a_part[:, 5:6], ALU.add))
                for r in range(NT):
                    last = nc.vector.tensor_tensor(e_const[:, r, 0:1], a_part[:, 6:7], a_part[:, 7:8], ALU.add)
                then(last)
                for r in range(NT):
                    nc.vector.tensor_scalar(e_const[:, r, 1:2], e_const[:, r, 0:1], 0.2, None, ALU.mult)
                for n in range(2, HOPS):
                    then(nc.vector.tensor_tensor(bk_row[:, :], bk_row[:, :], hid_rows[n], ALU.add))
                dve.drain().then_inc(s_split, 1)

            nc.vector.memset(vqk0[:, :, D + 2 * Q0:], 1.0)
            nc.vector.memset(ones[:, :], 1.0).then_inc(s_ones, 1)
            dve.wait_ge(s_ones, 1)
            for r in range(NT):
                nc.vector.tensor_copy(xw2_hl[:, 0, r, D:D + 2], ones[:, 0:2])
                nc.vector.tensor_tensor(xw2_hl[:, 1, r, D:D + 2], ones[:, 0:2], ones[:, 0:2], ALU.subtract)
                nc.vector.memset(e_const[:, r, 2:3], 0.0)
            for n in range(2):
                nc.vector.memset(v_heads[:, n, :, :, HD:HE], 1.0)

            def stat(n, src):
                for r in range(NT):
                    nc.vector.bn_stats(stats[n][:, r, :], src[:, r, :]).then_inc(s_stats[n], 1)

            def moment(n):
                for r in range(NT):
                    last = nc.vector.bn_aggr(moments[n][:, r, :], stats[n][:, r, :])
                last.then_inc(s_mean[n], 1)

            def normalise(n, src):
                for r in range(NT):
                    last = nc.vector.tensor_scalar(x_norm[n // 2][:, r, :], src[:, r, :], moments[n][:, r, 0:1],
                                                   rstd[n][:, r:r + 1], ALU.subtract, ALU.mult)
                last.then_inc(s_norm[n], 1)

            def relu_lo(n, src):
                hl = xt_hl[n // 2]
                nc.vector.scalar_tensor_tensor(out=flat(hl[:, 1]), in0=src[:, :], scalar=0.0, in1=flat(hl[:, 0]).bitcast(F32),
                                               op0=ALU.max, op1=ALU.subtract).then_inc(s_xt[n], 1)

            def bias_lo(hl, col, done):
                for k in range(KT):
                    last = nc.vector.scalar_tensor_tensor(
                        out=hl[:, 1, k, :], in0=tiles(bank_a[col])[:, k], scalar=bqk_col[:, col, k:k + 1],
                        in1=hl[:, 0, k, :].bitcast(F32), op0=ALU.add, op1=ALU.subtract)
                last.then_inc(done, 1)

            def scaled_add(dst, src, scale, more, done):
                for r in range(NT):
                    last = nc.vector.scalar_tensor_tensor(out=dst[:, r, :], in0=src[:, r, :], scalar=scale[:, r:r + 1],
                                                          in1=more[:, r, :], op0=ALU.mult, op1=ALU.add)
                last.then_inc(done, 1)

            def mask(g, h):
                for r in range(NT):
                    last = nc.vector.tensor_tensor_reduce(
                        masked[:, h % 3, r * N:(r + 1) * N], tiles(bank_s)[:, r], adj_n[:, g.four, r, :],
                        SCALE1, LEAST, ALU.mult, ALU.max, s_top[:, h % 3, r:r + 1])
                last.then_inc(s_masked, 1)

            def iteration(i, t):
                for s in range(SLOTS):
                    if isinstance(i, int) and t * SLOTS + s in SPLIT_AT:
                        n = SPLIT_AT.index(t * SLOTS + s)
                        weight_lo(n, list(w_src)[n])
                    if isinstance(i, int) and t * SLOTS + s == EDGE_WEIGHTS_AT:
                        edge_weights()
                    for slot, g in due(i, t, s):
                        if (h := head_at(slot, "masked")) is not None:
                            dve.wait_ge(s_scores, g.count(H, h + 1))
                            settled(dve)
                            mask(g, h)
                        if slot == SLOT["moments0"]:
                            dve.wait_ge(s_x[g.two], g.round(2, 16))
                            stat(0, x0[:, g.two])
                            dve.wait_ge(s_stats[0], g.count(NT, NT))
                            settled(dve)
                            moment(0)
                            dve.wait_ge(s_mean[0], g.count())
                            nc.vector.tensor_scalar(var_eps[0][:, :], moments[0][:, :, 1], 1e-5, None, ALU.add)\
                                .then_inc(s_moments[0], 1)
                        if slot == SLOT["norm0"]:
                            dve.wait_ge(s_rstd[0], g.count())
                            normalise(0, x0[:, g.two])
                        if slot == SLOT["xt0_lo"]:
                            dve.wait_ge(s_xt_hi[0], g.count())
                            relu_lo(0, bank_a[0])
                        if slot == SLOT["w_own"]:
                            dve.wait_ge(s_ak_ps, g.count())
                            settled(dve)
                            for r in range(NT):
                                nc.vector.tensor_tensor_reduce(qak[:, r, :], ak_ps[:, r, 0:Q0], vqk0[:, r, D:D + Q0], 1.0, 0.0,
                                                               ALU.mult, ALU.add, w_col[:, r:r + 1])
                            nc.vector.reciprocal(near_inv[:, g.four, :], ak_ps[:, :, Q0]).then_inc(s_w_col, 1)
                        if slot == SLOT["w_max"]:
                            dve.wait_ge(s_w_ps, g.count())
                            nc.vector.tensor_reduce(w_neg[:, 0:1], bank_a[1][:, 0:N], AX_X, ALU.max, negate=True)\
                                .then_inc(s_w_max, 1)
                            dve.wait_ge(s_w_max, g.count())
                            nc.vector.tensor_scalar(w_neg[:, 1:2], w_neg[:, 0:1], SCALE0, None, ALU.mult).then_inc(s_w_neg, 1)
                        if slot == SLOT["w_prob"]:
                            dve.wait_ge(s_w_exp, g.count())
                            nc.vector.reciprocal(w_sum[:, 1:2], w_sum[:, 0:1]).then_inc(s_w_inv, 1)
                            dve.wait_ge(s_w_inv, g.count())
                            nc.vector.tensor_scalar(w_prob[:, :], w_e[:, :], w_sum[:, 1:2], None, ALU.mult).then_inc(s_w_prob, 1)
                        if slot == SLOT["x1"]:
                            dve.wait_ge(s_w_prob, g.count())
                            scaled_add(x1, vqk0[:, :, 0:D], w_prob, x0[:, g.two], s_x1)
                            dve.wait_ge(s_x1, g.count())
                            stat(1, x1)
                            dve.wait_ge(s_stats[1], g.count(NT, NT))
                            settled(dve)
                            moment(1)
                            dve.wait_ge(s_mean[1], g.count())
                            nc.vector.tensor_scalar(var_eps[1][:, :], moments[1][:, :, 1], 1e-5, None, ALU.add)\
                                .then_inc(s_moments[1], 1)
                        if slot == SLOT["norm1"]:
                            dve.wait_ge(s_rstd[1], g.count())
                            normalise(1, x1)
                        if slot == SLOT["xt1_lo"]:
                            dve.wait_ge(s_xt_hi[1], g.count())
                            relu_lo(1, bank_a[0])
                        if slot == SLOT["q1_lo"]:
                            dve.wait_ge(s_q1_hi, g.count())
                            if g.first:
                                dve.wait_ge(s_biases, 16 * 5)
                            bias_lo(q_hl, 0, s_q1)
                        if slot == SLOT["k1_lo"]:
                            dve.wait_ge(s_k1_hi, g.count())
                            bias_lo(k_hl, 1, s_k1)
                        if slot == SLOT["v1"]:
                            dve.wait_ge(s_v1_ps, g.count())
                            for r in range(NT):
                                last = nc.vector.tensor_tensor(
                                    v_heads[:, g.two, r, :, 0:HD], tiles(bank_a[0])[:, r].rearrange("p (h e) -> p h e", h=H),
                                    bv_row[:, :].rearrange("p (h e) -> p h e", h=H), ALU.add)
                            last.then_inc(s_v1, 1)
                        if slot == SLOT["c_lo"]:
                            dve.wait_ge(s_c_hi, g.count())
                            nc.vector.tensor_tensor(c_hl[:, 1], tiles(bank_b), c_hl[:, 0].bitcast(F32), ALU.subtract)\
                                .then_inc(s_c, 1)
                        if slot == SLOT["x2"]:
                            dve.wait_ge(s_x2_ps, g.count())
                            dve.wait_ge(s_x1_bias, g.count())
                            nc.vector.tensor_tensor(x2[:, :, :], tiles(bank_b), x1_bias[:, g.four], ALU.add).then_inc(s_x2, 1)
                            dve.wait_ge(s_x2, g.count())
                            stat(2, x2)
                            dve.wait_ge(s_stats[2], g.count(NT, NT))
                            settled(dve)
                            moment(2)
                            dve.wait_ge(s_mean[2], g.count())
                            nc.vector.tensor_scalar(var_eps[2][:, :], moments[2][:, :, 1], 1e-5, None, ALU.add)\
                                .then_inc(s_moments[2], 1)
                        if slot == SLOT["norm2"]:
                            dve.wait_ge(s_rstd[2], g.count())
                            normalise(2, x2)
                        if slot == SLOT["xt2_lo"]:
                            dve.wait_ge(s_xt_hi[2], g.count())
                            relu_lo(2, bank_g[0])
                        if slot == SLOT["h2_lo"]:
                            dve.wait_ge(s_h2_hi, g.count())
                            nc.vector.tensor_tensor(h2_hl[:, 1], tiles(bank_g[0]), h2_hl[:, 0].bitcast(F32), ALU.subtract)\
                                .then_inc(s_h2, 1)
                        if slot == SLOT["x3"]:
                            dve.wait_ge(s_ah_ps, g.count())
                            dve.wait_ge(s_x2_bias, g.count())
                            if not g.first:
                                dve.wait_ge(s_out, g.before().count())
                            scaled_add(x3, tiles(bank_g[1]), near_inv[:, g.four], x2_bias, s_x3)
                            dve.wait_ge(s_x3, g.count())
                            stat(3, x3)
                            dve.wait_ge(s_stats[3], g.count(NT, NT))
                            settled(dve)
                            moment(3)
                            dve.wait_ge(s_mean[3], g.count())
                            nc.vector.tensor_scalar(var_eps[3][:, :], moments[3][:, :, 1], 1e-5, None, ALU.add)\
                                .then_inc(s_moments[3], 1)
                        if slot == SLOT["norm3"]:
                            dve.wait_ge(s_rstd[3], g.count())
                            normalise(3, x3)
                        if slot == SLOT["xt3_lo"]:
                            dve.wait_ge(s_xt_hi[3], g.count())
                            relu_lo(3, bank_g[0])
                        if slot == SLOT["xw2_lo"]:
                            dve.wait_ge(s_xw2_hi, g.count())
                            for r in range(NT):
                                nc.vector.tensor_tensor(xw2_hl[:, 1, r, 0:D], bank_g[r][:, 0:D],
                                                        xw2_hl[:, 0, r, 0:D].bitcast(F32), ALU.subtract)
                                last = nc.vector.tensor_tensor(e_bias[:, r, :], bank_g[r][:, D:D + 3], e_const[:, r, :], ALU.add)
                            last.then_inc(s_e_bias, 1)
                        if slot == SLOT["e_max"]:
                            dve.wait_ge(s_e, g.count())
                            nc.vector.tensor_tensor(e_max, e_pos, e_leak, ALU.max).then_inc(s_e_max, 1)
                        if slot == SLOT["y1"]:
                            dve.wait_ge(s_y2_ps, g.count())
                            for r in range(NT):
                                last = nc.vector.tensor_scalar(a_inv[:, 0, r:r + 1], bank_g[r][:, D:D + 1], 1e-12,
                                                               None, ALU.add)
                            last.then_inc(s_a_sum, 1)
                            dve.wait_ge(s_a_sum, g.count())
                            nc.vector.reciprocal(a_inv[:, 1, :], a_inv[:, 0, :]).then_inc(s_a_inv, 1)
                            dve.wait_ge(s_xw1, g.count())
                            dve.wait_ge(s_a_inv, g.count())
                            for r in range(NT):
                                last = nc.vector.scalar_tensor_tensor(
                                    out=y1[:, r, :], in0=bank_g[r][:, 0:D], scalar=a_inv[:, 1, r:r + 1],
                                    in1=xw1[:, r, :], op0=ALU.mult, op1=ALU.add)
                            last.then_inc(s_y1, 1)
                        if slot == SLOT["x_out"]:
                            dve.wait_ge(s_hop_ps, g.count())
                            dve.wait_ge(s_xw0_bias, g.count())
                            scaled_add(hid, tiles(bank_g[1]), a_inv[:, 1], xw0_bias, s_hid)
                            dve.wait_ge(s_hid, g.count())
                            if not g.first:
                                dve.wait_ge(s_stored, g.before().count(16, 16))
                            nc.vector.scalar_tensor_tensor(out=flat(x_out[:, :, :]), in0=flat(hid[:, :, :]), scalar=0.0,
                                                           in1=flat(x3[:, :, :]), op0=ALU.max, op1=ALU.add).then_inc(s_out, 1)
                        if slot in (SLOT["c_rows_first"], SLOT["c_rows_last"]):
                            part = int(slot == SLOT["c_rows_last"])
                            dve.wait_ge(s_context, g.count(H, (part + 1) * HG))
                            at = slice(part * HG, (part + 1) * HG)
                            nc.vector.reciprocal(c_inv[:, :, at], ctx_ps[:, :, :, HD]).then_inc(s_c_inv, 1)
                            dve.wait_ge(s_c_inv, g.count(2, part + 1))
                            per = HG // KT
                            for r in range(NT):
                                rows = c_rows[:, r].rearrange("p (t j) e -> p j t e", t=KT)
                                last = nc.vector.tensor_tensor(
                                    rows[:, part * per:(part + 1) * per],
                                    ctx_ps[:, r, :, 0:HD].rearrange("p (j t) e -> p j t e", t=KT),
                                    c_inv[:, r, at].rearrange("p (j t) -> p j t", t=KT).unsqueeze(3)
                                    .broadcast_to([P, per, KT, HD]), ALU.mult)
                            last.then_inc(s_c_rows, 1)

            for t in range(AHEAD):
                iteration(0, t)
            with dve.Fori(0, ROUNDS) as i:
                for u in range(BODY):
                    iteration(i, AHEAD + u)
            for t in range(ALL - BEHIND, ALL):
                iteration(0, t)

        @block.tensor
        def _(pe):
            def turn(dst, src):
                for k in range(2):
                    for r in range(2):
                        last = nc.tensor.transpose(dst[:, k * 256 + r * P:k * 256 + (r + 1) * P], src(r, k), ident[:, :])
                return last

            def split_product(dst, lhs, rhs):
                passes = [(k, p, q) for k in range(KT) for p, q in ((0, 0), (0, 1), (1, 0))]
                for n, (k, p, q) in enumerate(passes):
                    last = nc.tensor.matmul(dst, lhs(p, k), rhs(q, k), start=n == 0, stop=n == len(passes) - 1)
                return last

            def by_rows(dst, xt, w):
                for r in range(NT):
                    last = split_product(dst(r), lambda p, k: xt[:, p, k, r * P:(r + 1) * P], lambda q, k: w[:, q, k, :])
                return last

            def by_cols(dst, xt, w):
                for f in range(KT):
                    last = split_product(dst[:, f], lambda p, k: w[:, p, k, f * P:(f + 1) * P], lambda q, k: xt[:, q, k, :])
                return last

            def over_nodes(dst, lhs, rhs):
                for r in range(NT):
                    for k in range(NT):
                        last = nc.tensor.matmul(dst(r), lhs[:, k, r * P:(r + 1) * P], rhs(k), start=k == 0, stop=k == NT - 1)
                return last

            def across(dst, col):
                for r in range(NT):
                    last = nc.tensor.transpose(dst[:, r * P:(r + 1) * P], col(r).broadcast_to([P, P]), ident[:, :])
                return last

            def norm_t(n, dst):
                turn(dst, lambda r, k: x_norm[n // 2][:, r, k * P:(k + 1) * P]).then_inc(s_xt_ps[n], 1)

            def scores(g, h):
                for r in range(NT):
                    last = nc.tensor.matmul(tiles(bank_s)[:, r], q_stack[:, g.two, HEADS[h], r * P:(r + 1) * P],
                                            k_stack[:, g.two, HEADS[h], :], start=True, stop=True)
                last.then_inc(s_scores, 1)

            def context(g, h):
                for r in range(NT):
                    for k in range(NT):
                        last = nc.tensor.matmul(ctx_ps[:, r, h % HG, :], probs[:, h % 3, k * N + r * P:k * N + (r + 1) * P],
                                                v_heads[:, g.two, k, HEADS[h], :], start=k == 0, stop=k == NT - 1)
                last.then_inc(s_context, 1)

            def iteration(i, t):
                xa, xc = xt_hl
                rows_a, rows_g, rows_g1 = tiles(bank_a[0]), tiles(bank_g[0]), tiles(bank_g[1])
                for s in range(SLOTS):
                    for slot, g in due(i, t, s):
                        if (h := head_at(slot, "scores_mm")) is not None:
                            if h % KT == 0:
                                pe.wait_ge(s_stack[h // KT], g.count(STACK, STACK))
                            if not g.first or h > 0:
                                pe.wait_ge(s_masked, g.count(H, h))
                            scores(g, h)
                        if slot == SLOT["turn0"]:
                            if g.first:
                                pe.wait_ge(s_ident, 3)
                            else:
                                pe.wait_ge(s_v1, g.before().count())
                            pe.wait_ge(s_norm[0], g.count())
                            norm_t(0, bank_a[0])
                        if slot == SLOT["adj_turn"]:
                            if g.first:
                                pe.wait_ge(s_ident, 3)
                            else:
                                pe.wait_ge(s_k1, g.before().count())
                            pe.wait_ge(s_adj[g.four], g.round(4, 16))
                            turn(bank_a[1], lambda r, k: adj_n[:, g.four, r, k * P:(k + 1) * P]).then_inc(s_adj_ps, 1)
                        if slot == SLOT["v0_mm"]:
                            if g.first:
                                pe.wait_ge(s_split, 1)
                            pe.wait_ge(s_xt[0], g.count())
                            pe.wait_ge(s_adj_t, g.count())
                            by_rows(lambda r: bank_a[r][:, 0:D + 2 * Q0], xa, w_hl["v0"]).then_inc(s_v0_ps, 1)
                        if slot == SLOT["near_k_mm"]:
                            pe.wait_ge(s_vqk0, g.count())
                            over_nodes(lambda r: ak_ps[:, r], adj_t[:, g.four],
                                       lambda k: vqk0[:, k, D + Q0:D + 2 * Q0 + 1]).then_inc(s_ak_ps, 1)
                        if slot == SLOT["w_all_mm"]:
                            pe.wait_ge(s_w_col, g.count())
                            across(bank_a[1], lambda r: w_col[:, r:r + 1]).then_inc(s_w_ps, 1)
                        if slot == SLOT["turn1"]:
                            pe.wait_ge(s_norm[1], g.count())
                            norm_t(1, bank_a[0])
                        if slot == SLOT["q1_mm"]:
                            if g.first:
                                pe.wait_ge(s_split, 4)
                            pe.wait_ge(s_xt[1], g.count())
                            by_cols(tiles(bank_a[0]), xa, w_hl["q1"]).then_inc(s_q1_ps, 1)
                        if slot == SLOT["k1_mm"]:
                            by_cols(tiles(bank_a[1]), xa, w_hl["k1"]).then_inc(s_k1_ps, 1)
                        if slot == SLOT["v1_mm"]:
                            pe.wait_ge(s_q1, g.count())
                            by_rows(lambda r: rows_a[:, r], xa, w_hl["v1"]).then_inc(s_v1_ps, 1)
                        if (h := head_at(slot, "scores_turn")) is not None:
                            pe.wait_ge(s_centred, g.count(H, h + 1))
                            if not g.first or h > 0:
                                pe.wait_ge(s_probs, g.count(H, h))
                            turn(bank_t, lambda r, k: centred[:, h % 3, r * N + k * P:r * N + (k + 1) * P])\
                                .then_inc(s_scores_t, 1)
                        if slot == SLOT["c_turn"]:
                            pe.wait_ge(s_c_rows, g.count(2, 2))
                            if not g.first:
                                pe.wait_ge(s_x2, g.before().count())
                            turn(bank_b, lambda r, k: c_rows[:, r, k * HG:(k + 1) * HG, :].rearrange("p h e -> p (h e)"))\
                                .then_inc(s_cols_ps, 1)
                        if slot == SLOT["x2_mm"]:
                            if g.first:
                                pe.wait_ge(s_split, len(w_src) + 1)
                            pe.wait_ge(s_c, g.count())
                            by_rows(lambda r: tiles(bank_b)[:, r], c_hl, w_hl["o1"]).then_inc(s_x2_ps, 1)
                        if slot == SLOT["turn2"]:
                            if not g.first:
                                pe.wait_ge(s_xw0, g.before().count())
                            pe.wait_ge(s_norm[2], g.count())
                            norm_t(2, bank_g[0])
                        if slot == SLOT["h2_mm"]:
                            pe.wait_ge(s_xt[2], g.count())
                            by_rows(lambda r: rows_g[:, r], xc, w_hl["n2"]).then_inc(s_h2_ps, 1)
                        if slot == SLOT["x3_mm"]:
                            if not g.first:
                                pe.wait_ge(s_hid, g.before().count())
                            pe.wait_ge(s_h2, g.count())
                            pe.wait_ge(s_adj_hl, g.count())
                            by_rows(lambda r: rows_g1[:, r], adj_hl, h2_hl).then_inc(s_ah_ps, 1)
                        if slot == SLOT["turn3"]:
                            pe.wait_ge(s_norm[3], g.count())
                            norm_t(3, bank_g[0])
                        if slot == SLOT["xw2_mm"]:
                            pe.wait_ge(s_xt[3], g.count())
                            by_rows(lambda r: bank_g[r][:, 0:D + 4], xc, w_hl["h2"]).then_inc(s_xw2_ps, 1)
                        if slot == SLOT["edge_mm"]:
                            pe.wait_ge(s_e_bias, g.count())
                            across(bank_g[0], lambda r: e_bias[:, r, 2:3]).then_inc(s_e_ps, 1)
                        if slot == SLOT["xw1_mm"]:
                            pe.wait_ge(s_e_bias, g.count())
                            by_rows(lambda r: rows_g1[:, r], xc, w_hl["h1"]).then_inc(s_xw1_ps, 1)
                        if slot == SLOT["y1_mm"]:
                            pe.wait_ge(s_xw1, g.count())
                            pe.wait_ge(s_alpha_hl, g.count())
                            by_rows(lambda r: bank_g[r][:, 0:D + 2], alpha_hl, xw2_hl).then_inc(s_y2_ps, 1)
                        if slot == SLOT["xw0_mm"]:
                            pe.wait_ge(s_y1, g.count())
                            by_rows(lambda r: rows_g[:, r], xc, w_hl["h0"]).then_inc(s_xw0_ps, 1)
                        if slot == SLOT["hid_mm"]:
                            pe.wait_ge(s_y1_hl, g.count())
                            by_rows(lambda r: rows_g1[:, r], alpha_hl, y1_hl).then_inc(s_hop_ps, 1)
                        if (h := head_at(slot, "context_mm")) is not None:
                            pe.wait_ge(s_probs, g.count(H, h + 1))
                            if h == 0:
                                pe.wait_ge(s_v1, g.count())
                            if h == HG or h == 0 and not g.first:
                                pe.wait_ge(s_c_rows, g.count(2, h // HG))
                            context(g, h)

            for t in range(AHEAD):
                iteration(0, t)
            with pe.Fori(0, ROUNDS) as i:
                for u in range(BODY):
                    iteration(i, AHEAD + u)
            for t in range(ALL - BEHIND, ALL):
                iteration(0, t)


_OUT = (32, 256, 256)


def kernel(**inputs):
    import numpy as _np
    import concourse.bacc as _bacc
    from concourse import mybir as _mybir
    from concourse.bass_utils import run_bass_kernel_spmd as _run

    turned = {"L0_gnn_W_qk", "L0_gnn_W_v", "L1_gnn_Wq", "L1_gnn_Wk", "L1_gnn_Wv", "L1_gnn_Wo"}
    order = ["x", "adj", "L0_gnn_W_qk", "L0_gnn_W_v", "L1_gnn_Wq", "L1_gnn_bq", "L1_gnn_Wk", "L1_gnn_bk",
             "L1_gnn_Wv", "L1_gnn_bv", "L1_gnn_Wo", "L1_gnn_bo", "L2_gnn_W", "L2_gnn_b", "L3_gnn_Wv",
             "L3_gnn_bv", "L3_gnn_aw", "L3_gnn_ab", "L3_gnn_Wk", "L3_gnn_bk"]
    nc = _bacc.Bacc("TRN2", target_bir_lowering=False, num_devices=1)
    arrays, args = {}, []
    for name in order:
        a = _np.asarray(inputs[name])
        a = _np.ascontiguousarray(a.T if name in turned else a)
        arrays[f"in_{name}"] = a
        args.append(nc.dram_tensor(f"in_{name}", a.shape, _mybir.dt.from_np(a.dtype), kind="ExternalInput").ap())
    args.append(nc.dram_tensor("out_x", _OUT, _mybir.dt.float32, kind="ExternalOutput").ap())
    graph_layers_kernel(nc, *args)
    r = _run(nc, [arrays], core_ids=[0])
    return r.results[0]["out_x"]
```
